# Optimizing a Trainium2 kernel written in Bass

```python
import numpy as np
import jax
import jax.numpy as jnp

def _softmax(x, axis=-1):
    return jax.nn.softmax(x, axis=axis)

def _gelu(x):
    return jax.nn.gelu(x, approximate=True)

def _silu(x):
    return jax.nn.silu(x)

def _sigmoid(x):
    return jax.nn.sigmoid(x)

def _layernorm(x, axis=-1, eps=1e-05):
    m = jnp.mean(x, axis=axis, keepdims=True)
    v = jnp.var(x, axis=axis, keepdims=True)
    return (x - m) / jnp.sqrt(v + eps)

def _scatter_add(tgt, idx, src, axis=0):
    return tgt.at[idx].add(src)

def _segment_sum(src, seg, n):
    return jax.ops.segment_sum(src, seg, n)
kernel_name = 'mk_prb_d1_jaxref_r4_e2b38f'

def setup_inputs(seed: int=0):
    np.random.seed(seed)
    _w = jnp.asarray

    def _L0_attn_setup():
        import jax, jax.numpy as jnp
        import numpy as np
        B, L, D, H = (2, 512, 512, 16)
        DH = D // H
        EPS = 1e-05

        def _delta_rule(q, k, v, beta):

            def step(S, inp):
                qt, kt, vt, bt = inp
                v_pred = jnp.einsum('bhk,bhkv->bhv', kt, S)
                delta = (vt - v_pred) * bt[..., None]
                S = S + kt[..., None] * delta[:, :, None, :]
                ot = jnp.einsum('bhk,bhkv->bhv', qt, S)
                return (S, ot)
            xs = (q.transpose(2, 0, 1, 3), k.transpose(2, 0, 1, 3), v.transpose(2, 0, 1, 3), beta.transpose(2, 0, 1))
            S0 = jnp.zeros(q.shape[:2] + (q.shape[-1], v.shape[-1]), q.dtype)
            _, o = jax.lax.scan(step, S0, xs)
            return o.transpose(1, 2, 0, 3)
        key = jax.random.key(seed)
        ks = jax.random.split(key, 6)
        s = 0.02
        return {'hidden_states': jax.random.normal(ks[0], (B, L, D), jnp.float32), 'Wq': jax.random.normal(ks[1], (D, D), jnp.float32) * s, 'Wk': jax.random.normal(ks[2], (D, D), jnp.float32) * s, 'Wv': jax.random.normal(ks[3], (D, D), jnp.float32) * s, 'Wb': jax.random.normal(ks[4], (D, H), jnp.float32) * s, 'o_norm_weight': jnp.ones((DH,), jnp.float32), 'Wo': jax.random.normal(ks[5], (D, D), jnp.float32) * s}
    _L0_attn_in = _L0_attn_setup()

    def _L0_ffn_setup():
        import jax, jax.numpy as jnp
        import numpy as np
        B, S, H, I = (1, 64, 512, 1536)

        def _quantized_matmul(x, w, scale):
            wq = w.astype(jnp.float8_e4m3fn).astype(x.dtype)
            y = jnp.einsum('bsi,io->bso', x, wq)
            return y * scale
        key = jax.random.key(seed)
        ks = jax.random.split(key, 7)
        return {'x': jax.random.normal(ks[0], (B, S, H), dtype=jnp.float32), 'gate_w': jax.random.normal(ks[1], (H, I), dtype=jnp.float32) * 0.02, 'up_w': jax.random.normal(ks[2], (H, I), dtype=jnp.float32) * 0.02, 'down_w': jax.random.normal(ks[3], (I, H), dtype=jnp.float32) * 0.02, 'gate_scale': jax.random.uniform(ks[4], (I,), dtype=jnp.float32, minval=0.5, maxval=1.5), 'up_scale': jax.random.uniform(ks[5], (I,), dtype=jnp.float32, minval=0.5, maxval=1.5), 'down_scale': jax.random.uniform(ks[6], (H,), dtype=jnp.float32, minval=0.5, maxval=1.5)}
    _L0_ffn_in = _L0_ffn_setup()
    _d = {'L0_attn_hidden_states': _L0_attn_in['hidden_states'], 'L0_attn_Wq': _L0_attn_in['Wq'], 'L0_attn_Wk': _L0_attn_in['Wk'], 'L0_attn_Wv': _L0_attn_in['Wv'], 'L0_attn_Wb': _L0_attn_in['Wb'], 'L0_attn_o_norm_weight': _L0_attn_in['o_norm_weight'], 'L0_attn_Wo': _L0_attn_in['Wo'], 'L0_ffn_gate_w': _L0_ffn_in['gate_w'], 'L0_ffn_up_w': _L0_ffn_in['up_w'], 'L0_ffn_down_w': _L0_ffn_in['down_w'], 'L0_ffn_gate_scale': _L0_ffn_in['gate_scale'], 'L0_ffn_up_scale': _L0_ffn_in['up_scale'], 'L0_ffn_down_scale': _L0_ffn_in['down_scale']}
    _x0 = _d['L0_attn_hidden_states']
    _d['L0_attn_hidden_states'] = jax.random.normal(jax.random.fold_in(jax.random.key(seed), 1), (2, 4096, 512), dtype=_x0.dtype)
    del _x0
    return _d

def reference(L0_attn_hidden_states, L0_attn_Wq, L0_attn_Wk, L0_attn_Wv, L0_attn_Wb, L0_attn_o_norm_weight, L0_attn_Wo, L0_ffn_gate_w, L0_ffn_up_w, L0_ffn_down_w, L0_ffn_gate_scale, L0_ffn_up_scale, L0_ffn_down_scale):

    def _L0_attn_ref(hidden_states, Wq, Wk, Wv, Wb, o_norm_weight, Wo):
        import jax, jax.numpy as jnp
        import numpy as np
        B, L, D, H = (2, 512, 512, 16)
        DH = D // H
        EPS = 1e-05

        def _delta_rule(q, k, v, beta):

            def step(S, inp):
                qt, kt, vt, bt = inp
                v_pred = jnp.einsum('bhk,bhkv->bhv', kt, S)
                delta = (vt - v_pred) * bt[..., None]
                S = S + kt[..., None] * delta[:, :, None, :]
                ot = jnp.einsum('bhk,bhkv->bhv', qt, S)
                return (S, ot)
            xs = (q.transpose(2, 0, 1, 3), k.transpose(2, 0, 1, 3), v.transpose(2, 0, 1, 3), beta.transpose(2, 0, 1))
            S0 = jnp.zeros(q.shape[:2] + (q.shape[-1], v.shape[-1]), q.dtype)
            _, o = jax.lax.scan(step, S0, xs)
            return o.transpose(1, 2, 0, 3)
        b, l, d = hidden_states.shape
        h = Wb.shape[1]
        dh = d // h
        q = hidden_states @ Wq
        k = hidden_states @ Wk
        v = jax.nn.silu(hidden_states @ Wv)

        def heads(x):
            return x.reshape(b, l, h, dh).transpose(0, 2, 1, 3)
        q, k, v = (heads(q), heads(k), heads(v))

        def l2n(x):
            n = jnp.sqrt(jnp.sum(x * x, axis=-1, keepdims=True))
            return x / jnp.maximum(n, 1e-12)
        q, k = (l2n(q), l2n(k))
        q = q * dh ** (-0.5)
        beta = jax.nn.sigmoid(hidden_states @ Wb).transpose(0, 2, 1)
        o = _delta_rule(q, k, v, beta)
        o = o.transpose(0, 2, 1, 3)
        o = o * jax.lax.rsqrt(jnp.mean(o * o, axis=-1, keepdims=True) + EPS)
        o = o * o_norm_weight
        return o.reshape(b, l, d) @ Wo

    def _L0_ffn_ref(x, gate_w, up_w, down_w, gate_scale, up_scale, down_scale):
        import jax, jax.numpy as jnp
        import numpy as np
        B, S, H, I = (1, 64, 512, 1536)

        def _quantized_matmul(x, w, scale):
            wq = w.astype(jnp.float8_e4m3fn).astype(x.dtype)
            y = jnp.einsum('bsi,io->bso', x, wq)
            return y * scale
        gate = jax.nn.silu(_quantized_matmul(x, gate_w, gate_scale))
        up = _quantized_matmul(x, up_w, up_scale)
        fuse = gate * up
        return _quantized_matmul(fuse, down_w, down_scale)
    x = L0_attn_hidden_states
    xn = _layernorm(x, axis=-1)
    x = x + _L0_attn_ref(xn, L0_attn_Wq, L0_attn_Wk, L0_attn_Wv, L0_attn_Wb, L0_attn_o_norm_weight, L0_attn_Wo) + _L0_ffn_ref(xn, L0_ffn_gate_w, L0_ffn_up_w, L0_ffn_down_w, L0_ffn_gate_scale, L0_ffn_up_scale, L0_ffn_down_scale)
    return x

_drawn_inputs = setup_inputs


def setup_inputs(seed=0):
    import zlib

    import numpy as np

    out = dict(_drawn_inputs(seed))
    spreads = {'L0_attn_o_norm_weight': (1.0, 0.2)}
    factors = {}
    for name, (base, spread) in spreads.items():
        noise = np.random.default_rng([zlib.crc32(name.encode()), seed]).standard_normal(out[name].shape)
        drawn = base * np.exp(spread * noise) if base else spread * noise
        out[name] = jnp.asarray(drawn.astype(out[name].dtype))
    for name, factor in factors.items():
        out[name] = (out[name] * factor).astype(out[name].dtype)
    return out
```

```python
import concourse.bass as bass
from concourse import mybir
from contextlib import ExitStack

BATCH, LENGTH, DM = 2, 4096, 512
HEADS, DH = 16, 32
INNER = 1536
P = 128
SPAN_B = 256
SPANS = LENGTH // SPAN_B
TOK = BATCH * SPAN_B
TILES = TOK // P
CHUNK = 32
STEPS = SPAN_B // CHUNK
BC = BATCH * STEPS
QUADS = P // DH
MS = HEADS // QUADS
KT_ = DM // P
IC = INNER // P
LN_EPS = O_EPS = 1e-05

JOB_B, JOB_WO, JOB_GU, JOB_DN = 0, 13, 17, 41
XT_BANKS = [1, 2, 3, 1]
DENSE, XT_FIRST = 49, 4
DONE_XT = 44
TILED = 40
DONE_UW, DONE_CHAIN = 8, 16
V_STEPS, P_STEPS = 89, 63


def done_dense(job):
    return job if job < JOB_DN + 3 else DENSE - 1


def delta_block_kernel(nc: bass.Bass, x: bass.AP, wq: bass.AP, wk: bass.AP, wv: bass.AP, wb: bass.AP,
                       onw: bass.AP, wo: bass.AP, gate_w: bass.AP, up_w: bass.AP, down_w: bass.AP,
                       gate_s: bass.AP, up_s: bass.AP, down_s: bass.AP, out: bass.AP):
    F32, F16, BF16, I32 = mybir.dt.float32, mybir.dt.float16, mybir.dt.bfloat16, mybir.dt.int32
    ALU = mybir.AluOpType
    ACT = mybir.ActivationFunctionType
    AX = mybir.AxisListType.X

    x_v = x.rearrange("b (i h p) d -> b i p h d", h=2, p=P)
    out_v = out.rearrange("b (i h p) d -> b i p h d", h=2, p=P)

    ctx = ExitStack()
    with ctx:
        def sb(name, shape, dt=F32):
            return ctx.enter_context(nc.sbuf_tensor(name, shape, dt))

        def sem(name):
            return ctx.enter_context(nc.semaphore(name))

        w_hi = sb("w_hi", [P, KT_, 3 * DM + P], F16)
        w_lo = sb("w_lo", [P, KT_, 3 * DM + P], F16)
        wo_hi = sb("wo_hi", [P, MS, DM], F16)
        wo_lo = sb("wo_lo", [P, MS, DM], F16)
        wgu = sb("wgu", [P, KT_, 2 * INNER], F16)
        wd = sb("wd", [P, IC, DM], BF16)
        xs = sb("xs", [P, 2, TILES, DM])
        xt_hi = sb("xt_hi", [P, KT_, TOK], F16)
        xt_lo = sb("xt_lo", [P, KT_, TOK], F16)
        f_hi = sb("f_hi", [P, IC, TOK], F16)
        f_lo = sb("f_lo", [P, IC, TOK], F16)
        sg = sb("sg", [P, 2, TOK])
        fuse = sb("fuse", [P, 2, TOK])
        kt = sb("kt", [P, MS * BC, DH])
        qt = sb("qt", [P, MS * BC, DH])
        vt = sb("vt", [P, MS * BC, DH])
        kq = sb("kq", [P, MS * BC, 2, CHUNK])
        at = sb("at", [P, 2048])
        mt = sb("mt", [P, 2048])
        pt = sb("pt", [P, MS * BC, CHUNK])
        outer_v = sb("outer_v", [P, 256])
        outer_p = sb("outer_p", [P, 256])
        state = sb("state", [P, 2, BATCH, MS, DH])
        bt = sb("bt", [P, BC, CHUNK])
        tb = sb("tb", [P, MS, BC])
        beta = sb("beta", [P, MS * BC])
        ssk, ssq, sso = (sb(n, [P, MS * BC]) for n in ("ssk", "ssq", "sso"))
        rk, rq, ro = (sb(n, [P, MS * BC]) for n in ("rk", "rq", "ro"))
        stats = sb("stats", [P, TILES, 6])
        mv = sb("mv", [P, TILES, 2])
        var_e = sb("var_e", [P, TILES])
        rstd = sb("rstd", [P, TILES])
        ident = sb("ident", [P, P])
        causal = sb("causal", [P, CHUNK])
        ones = sb("ones", [P, 1])
        neg_half = sb("neg_half", [P, MS * BC])
        pos_half = sb("pos_half", [P, IC])
        gs = sb("gs", [P, IC])
        us = sb("us", [P, IC])
        usf = sb("usf", [P, IC])
        row_inv = sb("row_inv", [P, IC])
        row_fs = sb("row_fs", [P, IC])
        bound = sb("bound", [P, 2 * IC])
        b_a = sb("b_a", [P, IC])
        b_b = sb("b_b", [P, IC])
        ds_row = sb("ds_row", [P, DM])
        onw4 = sb("onw4", [P, 1])
        wb_raw = sb("wb_raw", [P, KT_, HEADS])
        amax = sb("amax", [P, 5])
        amax_all = sb("amax_all", [P, 5])
        amax_e = sb("amax_e", [P, 5])
        w_scale = sb("w_scale", [P, 5])
        w_inv = sb("w_inv", [P, 5])

        D = [ctx.enter_context(nc.psum_tensor(f"D{b}", [P, 512], F32)) for b in range(4)]
        E = [ctx.enter_context(nc.psum_tensor(f"E{b}", [P, 512], F32)) for b in range(2)]
        F = [ctx.enter_context(nc.psum_tensor(f"F{b}", [P, 512], F32)) for b in range(2)]

        a_nat = at[:, :].rearrange("p (g n s) -> p g n s", g=2, n=32)
        t_prob = at[:, :].rearrange("p (g i c) -> p g i c", g=2, i=CHUNK)
        m_prob = mt[:, :].rearrange("p (g j i) -> p g j i", g=2, j=CHUNK)
        tt = mt[:, :].rearrange("p (n t) -> p n t", t=CHUNK)
        xn = at[:, :].rearrange("p (j d) -> p j d", j=TILES)
        o_split = mt[:, :].bitcast(F16).rearrange("p (s m n) -> p s m n", s=2, m=MS)
        kq_flat = kq[:, :, :, :].rearrange("p n a t -> p (n a t)")
        o_t = kq_flat[:, 0:2048].rearrange("p (m n) -> p m n", m=MS)
        u_v = vt[:, :, :].rearrange("p (m b c) d -> p b c m d", m=MS, b=BATCH)
        o_v = qt[:, :, :].rearrange("p (m b c) d -> p b c m d", m=MS, b=BATCH)
        sq_acc = f_hi[:, :, :].rearrange("p a b -> p (a b)").bitcast(F32)
        raw = [kq_flat[:, 0:INNER], kq_flat[:, INNER:2 * INNER]]
        magic = [at[:, 0:INNER], mt[:, 0:INNER]]
        vt_flat = vt[:, :, :].rearrange("p n d -> p (n d)")

        dense_done, tiled_done = sem("dense_done"), sem("tiled_done")
        x_loaded, y_stored = sem("x_loaded"), sem("y_stored")
        w_loaded = [sem(f"w_loaded{n}") for n in range(5)]
        small_loaded = sem("small_loaded")
        stage_loaded = [sem(f"stage_loaded{n}") for n in range(2)]
        wd_ready = sem("wd_ready")
        consts = sem("consts")
        amax_ready, amax_summed, scales_ready = sem("amax_ready"), sem("amax_summed"), sem("scales_ready")
        hi_ready, proj_ready = sem("hi_ready"), sem("proj_ready")
        wgu_ready, sq_ready, sq_added = sem("wgu_ready"), sem("sq_ready"), sem("sq_added")
        norms_full, bound2_ready, bound_ready, ffn_ready = (
            sem("norms_full"), sem("bound2_ready"), sem("bound_ready"), sem("ffn_ready"))
        set_v = sem("set_v")
        var_ready, rstd_ready, xn_ready = sem("var_ready"), sem("rstd_ready"), sem("xn_ready")
        xt_hi_ready, xt_lo_ready = sem("xt_hi_ready"), sem("xt_lo_ready")
        k_raw, q_raw, v_raw, b_raw = sem("k_raw"), sem("q_raw"), sem("v_raw"), sem("b_raw")
        k_sq, q_sq, tb_ready, v_ready = sem("k_sq"), sem("q_sq"), sem("tb_ready"), sem("v_ready")
        ssk_ready, ssq_ready, rk_pow, rq_pow = sem("ssk_ready"), sem("ssq_ready"), sem("rk_pow"), sem("rq_pow")
        rk_ready, kn_ready, kq_ready = sem("rk_ready"), sem("kn_ready"), sem("kq_ready")
        m_ready, t0_ready, tt_ready, p_ready = sem("m_ready"), sem("t0_ready"), sem("tt_ready"), sem("p_ready")
        u_ready, w_ready, r_ready, s_ready = sem("u_ready"), sem("w_ready"), sem("r_ready"), sem("s_ready")
        sg_ready, f_ready, fhi_ready, flo_ready = sem("sg_ready"), sem("f_ready"), sem("fhi_ready"), sem("flo_ready")
        dn_ready, acc_ready, wo_added = sem("dn_ready"), sem("acc_ready"), sem("wo_added")
        o_ready, o_sq, sso_ready, ro_pow = sem("o_ready"), sem("o_sq"), sem("sso_ready"), sem("ro_pow")
        ot_ready, ohi_ready, olo_ready = sem("ot_ready"), sem("ohi_ready"), sem("olo_ready")
        v_step, p_step = sem("v_step"), sem("p_step")

        def at_span(it, par, per_span, n=0):
            return it * (2 * per_span) + (par * per_span + n)

        block = ctx.enter_context(nc.Block())

        @block.sync
        def _(sp):
            for b in range(BATCH):
                sp.dma_start(xs[:, 0, 2 * b:2 * b + 2, :], x_v[b, 0]).then_inc(x_loaded, 16)
            for n, (dst, src) in enumerate(((qt, wq), (kt, wk), (vt, wv))):
                sp.dma_start(dst[:, :, :].rearrange("p n d -> p (n d)").rearrange("p (k c) -> p k c", k=KT_),
                             src.rearrange("(k p) c -> p k c", p=P)).then_inc(w_loaded[n], 16)
            sp.dma_start(wb_raw[:, :, :], wb.rearrange("(k p) c -> p k c", p=P)).then_inc(w_loaded[3], 16)
            sp.dma_start(pt[:, :, :].rearrange("p n d -> p (n d)").rearrange("p (k c) -> p k c", k=KT_),
                         wo.rearrange("(k p) c -> p k c", p=P)).then_inc(w_loaded[4], 16)
            for h in range(QUADS):
                sp.dma_start(onw4[32 * h:32 * h + 32, :], onw.rearrange("(d o) -> d o", o=1), allow_slow_non_contiguous=True).then_inc(small_loaded, 16)
            sp.dma_start(gs[:, :], gate_s.rearrange("(c p) -> p c", p=P), allow_slow_non_contiguous=True).then_inc(small_loaded, 16)
            sp.dma_start(us[:, :], up_s.rearrange("(c p) -> p c", p=P), allow_slow_non_contiguous=True).then_inc(small_loaded, 16)
            sp.dma_start(ds_row[:, :], down_s.partition_broadcast(P)).then_inc(small_loaded, 16)
            for n in range(12):
                if n >= 2:
                    if n - 2 < 8:
                        sp.wait_ge(wgu_ready, n - 1)
                    else:
                        sp.wait_ge(wd_ready, n - 9)
                if n < 8:
                    src = (gate_w, up_w)[n % 2][(n // 2) * P:(n // 2 + 1) * P, :]
                    sp.dma_start(raw[n % 2], src).then_inc(stage_loaded[n % 2], 16)
                else:
                    r = 3 * (n - 8) * P
                    sp.dma_start(raw[n % 2].rearrange("p (c d) -> p c d", c=3),
                                 down_w[r:r + 3 * P, :].rearrange("(c p) d -> p c d", p=P)).then_inc(stage_loaded[n % 2], 16)

            def load_x(span, par):
                for b in range(BATCH):
                    sp.dma_start(xs[:, par, 2 * b:2 * b + 2, :], x_v[b, span]).then_inc(x_loaded, 16)

            def store_y(span, par):
                for b in range(BATCH):
                    sp.dma_start(out_v[b, span], xs[:, par, 2 * b:2 * b + 2, :]).then_inc(y_stored, 16)

            sp.wait_ge(wo_added, TILES)
            load_x(1, 1)
            with sp.Fori(0, (SPANS - 2) // 2) as it:
                for par in range(2):
                    sp.wait_ge(wo_added, at_span(it, par, TILES, 2 * TILES))
                    sp.nop(nofuse=True)
                    store_y(it * 2 + par, par)
                    sp.wait_ge(y_stored, at_span(it, par, 32, 32))
                    sp.nop(nofuse=True)
                    load_x(it * 2 + (par + 2), par)
            sp.wait_ge(wo_added, TILES * SPANS)
            store_y(SPANS - 2, 0)
            sp.wait_ge(y_stored, 32 * (SPANS - 1))
            load_x(0, 0)
            sp.wait_ge(wo_added, TILES * (SPANS + 1))
            store_y(SPANS - 1, 1)
            sp.wait_ge(y_stored, 32 * SPANS)
            sp.wait_ge(x_loaded, 32 * (SPANS + 1))

        @block.tensor
        def _(pe):
            def quads(out, lhs, rhs, start=True, stop=True):
                for h in range(QUADS):
                    s = slice(32 * h, 32 * h + 32)
                    last = nc.tensor.matmul(out[s], lhs[s], rhs[s], start=start, stop=stop)
                return last

            def transpose_xn(j, bank):
                for k in range(KT_):
                    last = nc.tensor.transpose(D[bank][:, k * P:(k + 1) * P], xn[:, j, k * P:(k + 1) * P], ident[:, :])
                last.then_inc(dense_done, 1)

            def project_out(j, bank):
                n = 0
                for m in range(MS):
                    for o_part, w in ((0, wo_hi), (1, wo_hi), (0, wo_lo)):
                        last = nc.tensor.matmul(D[bank][:, :], o_split[:, o_part, m, j * P:(j + 1) * P], w[:, m, :],
                                                start=n == 0, stop=n == 3 * MS - 1)
                        n += 1
                last.then_inc(dense_done, 1)

            pe.wait_ge(consts, 2)
            for j in range(TILES):
                b = XT_BANKS[j]
                pe.wait_ge(xn_ready, j + 1)
                if j == 3:
                    pe.wait_ge(xt_lo_ready, 1)
                transpose_xn(j, b)
            pe.wait_ge(sq_added, 8)
            for c in range(2 * IC):
                last = nc.tensor.matmul(F[0][:, c:c + 1], sq_acc[:, c * P:(c + 1) * P], ones[:, :], start=True, stop=True)
            last.then_inc(norms_full, 1)
            pe.wait_ge(proj_ready, 5)
            pe.wait_ge(ffn_ready, 1)

            def two_spans(it):
                for par in range(2):
                    def since(per_span, n=0):
                        return at_span(it, par, per_span, n)

                    def take(job):
                        before = job - 4
                        if before < 0:
                            pe.wait_ge(*((dn_ready, since(TILES)) if job == 0 else (xt_lo_ready, since(TILES, TILES))))
                        elif before < 4:
                            pe.wait_ge(k_raw, since(MS, before + 1))
                        elif before < 8:
                            pe.wait_ge(q_raw, since(MS, before - 3))
                        elif before < 9:
                            pe.wait_ge(b_raw, since(1, 1))
                        elif before < JOB_WO:
                            pe.wait_ge(v_raw, since(MS, before - 8))
                        elif before < JOB_GU:
                            pe.wait_ge(wo_added, since(TILES, before - JOB_WO + 1))
                        else:
                            ic, up = divmod(before - JOB_GU, 2)
                            pe.wait_ge(f_ready if up else sg_ready, since(IC, ic + 1))
                        return job % 4

                    pe.wait_ge(xt_lo_ready, since(TILES, TILES))
                    for job in range(13):
                        g = (4, 5, 6, 7, 0, 1, 2, 3, 12, 8, 9, 10, 11)[job]
                        bank = take(JOB_B + job)
                        cols = slice(g * P, (g + 1) * P)
                        n = 0
                        for k in range(KT_):
                            for w, xp in ((w_hi, xt_hi), (w_hi, xt_lo), (w_lo, xt_hi)):
                                last = nc.tensor.matmul(D[bank][:, :], w[:, k, cols], xp[:, k, :],
                                                        start=n == 0, stop=n == 3 * KT_ - 1)
                                n += 1
                        last.then_inc(dense_done, 1)
                    pe.wait_ge(olo_ready, since(1, 0))
                    for j in range(TILES):
                        project_out(j, take(JOB_WO + j))

                    def gate_up(ic):
                        for side in range(2):
                            bank = take(JOB_GU + 2 * ic + side)
                            c = side * INNER + ic * P
                            for k in range(KT_):
                                nc.tensor.matmul(D[bank][:, :], wgu[:, k, c:c + P], xt_hi[:, k, :], start=k == 0, stop=False)
                                last = nc.tensor.matmul(D[bank][:, :], wgu[:, k, c:c + P], xt_lo[:, k, :],
                                                        start=False, stop=k == KT_ - 1)
                            last.then_inc(dense_done, 1)

                    def gram(g):
                        e = g % 2
                        pe.wait_ge(kq_ready, since(MS, g // 2 + 1))
                        if g < 2:
                            pe.wait_ge((r_ready, s_ready)[g], since(STEPS))
                        else:
                            pe.wait_ge(p_ready, since(8, g - 1))
                        pe.nop(nofuse=True)
                        for n in range(8):
                            both = kq_flat.rearrange("p (n t) -> p n t", t=2 * CHUNK)[:, 8 * g + n, :]
                            last = quads(E[e][:, 64 * n:64 * n + 64], both[:, 0:CHUNK], both)
                        last.then_inc(tiled_done, 1)

                    for ic in range(IC):
                        gate_up(ic)
                        if 2 <= ic < 6:
                            gram(2 * (ic - 2))
                            gram(2 * (ic - 2) + 1)

                    pe.wait_ge(v_ready, since(1, 1))
                    for m in range(MS):
                        pe.wait_ge(tt_ready, since(2, m // 2 + 1))
                        pe.wait_ge(*((u_ready, since(MS, m)) if m else (p_ready, since(8, 7))))
                        pe.nop(nofuse=True)
                        for n in range(BC):
                            pc = m * BC + n
                            last = quads(E[0][:, 32 * n:32 * n + 32], tt[:, pc, :], vt[:, pc, :])
                        last.then_inc(tiled_done, 1)
                        pe.wait_ge(*((w_ready, since(MS, m)) if m else (p_ready, since(8, 8))))
                        pe.nop(nofuse=True)
                        for n in range(BC):
                            pc = m * BC + n
                            last = quads(E[1][:, 32 * n:32 * n + 32], kt[:, pc, :], tt[:, pc, :])
                        last.then_inc(tiled_done, 1)

                    def down(j, part):
                        bank = (JOB_DN + j) % 4
                        for ic in range(3 * part, 3 * part + 3):
                            nc.tensor.matmul(D[bank][:, :], f_hi[:, ic, j * P:(j + 1) * P], wd[:, ic, :], start=ic == 0, stop=False)
                            last = nc.tensor.matmul(D[bank][:, :], f_lo[:, ic, j * P:(j + 1) * P], wd[:, ic, :],
                                                    start=False, stop=ic == IC - 1)
                        if part == 3:
                            last.then_inc(dense_done, 1)

                    for c in range(STEPS):
                        s_old = state[:, c % 2]
                        if c == 0:
                            pe.wait_ge(w_ready, since(MS, MS))
                        pe.wait_ge(s_ready, since(STEPS, c))
                        pe.wait_ge(*((r_ready, since(STEPS, c)) if c else (u_ready, since(MS, MS))))
                        pe.nop(nofuse=True)
                        for b in range(BATCH):
                            for m in range(MS):
                                n = b * MS + m
                                last = quads(E[0][:, 32 * n:32 * n + 32], kq[:, m * BC + b * STEPS + c, 0, :], s_old[:, b, m, :])
                        last.then_inc(tiled_done, 1)
                        if c == 0:
                            pe.wait_ge(flo_ready, since(IC, IC))
                        if c % 2 == 0:
                            take(JOB_DN + c // 2)
                        down(c // 2, 2 * (c % 2))
                        pe.wait_ge(r_ready, since(STEPS, c + 1))
                        pe.nop(nofuse=True)
                        for b in range(BATCH):
                            for m in range(MS):
                                n, pc = b * MS + m, m * BC + b * STEPS + c
                                last = quads(E[1][:, 32 * n:32 * n + 32], kt[:, pc, :], vt[:, pc, :])
                        last.then_inc(tiled_done, 1)
                        if c == 0:
                            pe.wait_ge(p_ready, since(8, 8))
                        pe.wait_ge(o_ready, since(STEPS, max(0, c - 1)))
                        pe.nop(nofuse=True)
                        for b in range(BATCH):
                            for m in range(MS):
                                n, pc = b * MS + m, m * BC + b * STEPS + c
                                quads(F[c % 2][:, 32 * n:32 * n + 32], kq[:, pc, 1, :], s_old[:, b, m, :], stop=False)
                                last = quads(F[c % 2][:, 32 * n:32 * n + 32], pt[:, pc, :], vt[:, pc, :], start=False)
                        last.then_inc(tiled_done, 1)
                        down(c // 2, 2 * (c % 2) + 1)
                        if c == STEPS - 2:
                            for j in range(TILES):
                                pe.wait_ge(xn_ready, since(TILES, TILES + j + 1))
                                pe.wait_ge(*((dn_ready, since(TILES, j + 1)) if j < 3 else (xt_lo_ready, since(TILES, TILES + 1))))
                                transpose_xn(j, XT_BANKS[j])

            two_spans(0)
            with pe.Fori(1, SPANS // 2) as it:
                two_spans(it)

            pe.wait_ge(olo_ready, SPANS)
            pe.wait_ge(dn_ready, TILES * SPANS)
            pe.wait_ge(xt_lo_ready, TILES * (SPANS + 1))
            for j in range(TILES):
                project_out(j, j)

        @block.scalar
        def _(act):
            def evacuate_xt(j, bank):
                nc.scalar.activation(xt_hi[:, :, j * P:(j + 1) * P], D[bank][:, :].rearrange("p (k n) -> p k n", k=KT_),
                                     ACT.Copy).then_inc(xt_hi_ready, 1)

            for j in range(TILES):
                act.wait_ge(dense_done, j + 1)
                evacuate_xt(j, XT_BANKS[j])
            act.wait_ge(scales_ready, 1)
            for n, src in enumerate((qt, kt, vt)):
                nc.scalar.activation(w_hi[:, :, n * DM:(n + 1) * DM],
                                     src[:, :, :].rearrange("p n d -> p (n d)").rearrange("p (k c) -> p k c", k=KT_),
                                     ACT.Identity, scale=w_scale[:, n:n + 1]).then_inc(hi_ready, 1)
            nc.scalar.activation(wo_hi[:, :, :], pt[:, :, :].rearrange("p n d -> p (n d)").rearrange("p (k c) -> p k c", k=KT_),
                                 ACT.Identity, scale=w_scale[:, 4:5]).then_inc(hi_ready, 1)
            act.wait_ge(proj_ready, 5)
            for n in range(8):
                act.wait_ge(wgu_ready, n + 1)
                if n >= 1:
                    act.wait_ge(sq_added, n)
                nc.scalar.activation(vt_flat[:, 0:INNER], wgu[:, n // 2, (n % 2) * INNER:(n % 2 + 1) * INNER],
                                     ACT.Square).then_inc(sq_ready, 1)
            act.wait_ge(ffn_ready, 1)

            def two_spans(it):
                for par in range(2):
                    def since(per_span, n=0):
                        return at_span(it, par, per_span, n)

                    def full(job):
                        act.wait_ge(dense_done, since(DENSE, XT_FIRST + done_dense(job) + 1))
                        return job % 4

                    flat = lambda t: t[:, :, :].rearrange("p n d -> p (n d)")
                    act.wait_ge(k_raw, since(MS, MS))
                    nc.scalar.activation(at[:, :], flat(kt), ACT.Square, scale=w_inv[:, 1:2]).then_inc(k_sq, 1)
                    act.wait_ge(q_raw, since(MS, MS))
                    nc.scalar.activation(flat(pt), flat(qt), ACT.Square, scale=w_inv[:, 0:1]).then_inc(q_sq, 1)
                    act.wait_ge(b_raw, since(1, 1))
                    nc.scalar.activation(tb[:, :, :], bt[:, :, 0:MS].rearrange("p c m -> p m c"), ACT.Tanh,
                                         scale=w_inv[:, 3:4]).then_inc(tb_ready, 1)
                    act.wait_ge(v_raw, since(MS, MS))
                    nc.scalar.activation(flat(vt), flat(vt), ACT.Silu, scale=w_inv[:, 2:3]).then_inc(v_ready, 1)

                    def high_part(ic):
                        act.wait_ge(f_ready, since(IC, ic + 1))
                        nc.scalar.activation(f_hi[:, ic, :], fuse[:, ic % 2, :], ACT.Copy).then_inc(fhi_ready, 1)

                    for ic in range(IC):
                        bank = full(JOB_GU + 2 * ic)
                        nc.scalar.activation(sg[:, ic % 2, :], D[bank][:, :], ACT.Silu,
                                             scale=gs[:, ic:ic + 1]).then_inc(sg_ready, 1)
                        if ic:
                            high_part(ic - 1)
                    high_part(IC - 1)
                    for m in range(MS):
                        act.wait_ge(tiled_done, since(TILED, DONE_UW + 2 * m + 2))
                        nc.scalar.activation(kq[:, m * BC:(m + 1) * BC, 0, :], E[1][:, :].rearrange("p (n t) -> p n t", t=CHUNK),
                                             ACT.Copy).then_inc(w_ready, 1)
                    for c in range(STEPS):
                        act.wait_ge(tiled_done, since(TILED, DONE_CHAIN + 3 * c + 3))
                        nc.scalar.activation(o_v[:, :, c], F[c % 2][:, 0:256].rearrange("p (b m d) -> p b m d", b=BATCH, m=MS),
                                             ACT.Copy).then_inc(o_ready, 1)
                        if c == STEPS - 2:
                            for j in range(TILES):
                                act.wait_ge(dense_done, since(DENSE, XT_FIRST + DONE_XT + j + 1))
                                evacuate_xt(j, XT_BANKS[j])
                    act.wait_ge(o_ready, since(STEPS, STEPS))
                    nc.scalar.activation(flat(pt), flat(qt), ACT.Square).then_inc(o_sq, 1)
                    act.wait_ge(ot_ready, since(1, 1))
                    nc.scalar.activation(o_split[:, 0], o_t, ACT.Copy).then_inc(ohi_ready, 1)

            two_spans(0)
            with act.Fori(1, SPANS // 2) as it:
                two_spans(it)

        @block.gpsimd
        def _(pool):
            nc.gpsimd.memset(ident[:, :], 0.0).then_inc(consts, 1)
            pool.wait_ge(consts, 1)
            nc.gpsimd.affine_select(out=ident[:, :], in_=ident[:, :], compare_op=ALU.not_equal, fill=1.0, base=0,
                                    pattern=[[-1, P]], channel_multiplier=1).then_inc(consts, 1)
            nc.gpsimd.memset(neg_half[:, :], -0.5)
            nc.gpsimd.memset(pos_half[:, :], 0.5)
            nc.gpsimd.memset(ones[:, :], 1.0)
            nc.gpsimd.memset(sq_acc, 0.0)
            nc.gpsimd.memset(causal[:, :], 1.0).then_inc(consts, 1)
            pool.wait_ge(consts, 3)
            for h in range(QUADS):
                c = causal[32 * h:32 * h + 32, :]
                nc.gpsimd.affine_select(out=c, in_=c, compare_op=ALU.is_ge, fill=0.0, base=0,
                                        pattern=[[1, CHUNK]], channel_multiplier=-1).then_inc(consts, 1)
                pool.wait_ge(consts, 4 + h)
            pool.wait_ge(var_ready, 1)
            nc.gpsimd.tensor_tensor(rstd[:, :], var_e[:, :], neg_half[:, 0:TILES], ALU.pow).then_inc(rstd_ready, 1)
            pool.wait_ge(amax_ready, 5)
            nc.gpsimd.partition_all_reduce(amax_all[:, :], amax[:, :], P, bass.bass_isa.ReduceOp.absmax).then_inc(amax_summed, 1)
            for n in range(8):
                acc = sq_acc[:, (n % 2) * INNER:(n % 2 + 1) * INNER]
                pool.wait_ge(sq_ready, n + 1)
                if n:
                    pool.wait_ge(sq_added, n)
                nc.gpsimd.tensor_tensor(acc, acc, vt_flat[:, 0:INNER], ALU.add).then_inc(sq_added, 1)
            pool.wait_ge(bound2_ready, 1)
            nc.gpsimd.tensor_tensor(b_b[:, :], b_a[:, :], pos_half[:, :], ALU.pow).then_inc(bound_ready, 1)
            pool.wait_ge(ffn_ready, 1)

            def two_spans(it):
                for par in range(2):
                    def since(per_span, n=0):
                        return at_span(it, par, per_span, n)

                    steps = [0]

                    def step(ins):
                        ins.then_inc(p_step, 1)
                        steps[0] += 1

                    def after_last():
                        pool.wait_ge(p_step, since(P_STEPS, steps[0]))

                    pool.wait_ge(ssk_ready, since(1, 1))
                    nc.gpsimd.tensor_tensor(rk[:, :], ssk[:, :], neg_half[:, :], ALU.pow).then_inc(rk_pow, 1)
                    pool.wait_ge(rk_ready, since(1, 1))
                    nc.gpsimd.tensor_tensor(kt[:, :, :], kt[:, :, :], rk[:, :].unsqueeze(2).to_broadcast([P, MS * BC, DH]),
                                            ALU.mult).then_inc(kn_ready, 1)
                    pool.wait_ge(ssq_ready, since(1, 1))
                    nc.gpsimd.tensor_tensor(rq[:, :], ssq[:, :], neg_half[:, :], ALU.pow).then_inc(rq_pow, 1)

                    def low_part(ic):
                        pool.wait_ge(fhi_ready, since(IC, ic + 1))
                        pool.nop(nofuse=True)
                        nc.gpsimd.tensor_tensor(f_lo[:, ic, :], fuse[:, ic % 2, :], f_hi[:, ic, :],
                                                ALU.subtract).then_inc(flo_ready, 1)

                    for ic in range(6):
                        low_part(ic)
                    T, M = t_prob[:, 0], m_prob[:, 0]
                    pool.wait_ge(m_ready, since(2, 1))
                    pool.nop(nofuse=True)
                    step(nc.gpsimd.memset(at[:, 0:1024], 0.0))
                    after_last()
                    pool.nop(nofuse=True)
                    step(nc.gpsimd.memset(at[:, 0:1024:CHUNK + 1], 1.0))
                    for j in range(CHUNK - 1):
                        rows, cols = CHUNK - 1 - j, j + 1
                        tmp = outer_p[:, 0:rows * cols].rearrange("p (i c) -> p i c", c=cols)
                        after_last()
                        step(nc.gpsimd.tensor_tensor(tmp, M[:, j, j + 1:].unsqueeze(2).to_broadcast([P, rows, cols]),
                                                     T[:, j, 0:cols].unsqueeze(1).to_broadcast([P, rows, cols]), ALU.mult))
                        after_last()
                        ins = nc.gpsimd.tensor_tensor(T[:, j + 1:, 0:cols], T[:, j + 1:, 0:cols], tmp, ALU.subtract)
                        if j < CHUNK - 2:
                            step(ins)
                        else:
                            ins.then_inc(t0_ready, 1)
                        if j % 5 == 4:
                            low_part(6 + j // 5)
                    assert steps[0] == P_STEPS, steps

                    def add_down(j):
                        pool.wait_ge(dn_ready, since(TILES, j + 1))
                        pool.nop(nofuse=True)
                        nc.gpsimd.tensor_tensor(xs[:, par, j, :], xs[:, par, j, :], fuse[:, j % 2, :], ALU.add).then_inc(acc_ready, 1)

                    pool.wait_ge(var_ready, since(1, 2))
                    nc.gpsimd.tensor_tensor(rstd[:, :], var_e[:, :], neg_half[:, 0:TILES], ALU.pow).then_inc(rstd_ready, 1)
                    for j in range(TILES):
                        add_down(j)
                    pool.wait_ge(sso_ready, since(1, 1))
                    nc.gpsimd.tensor_tensor(ro[:, :], sso[:, :], neg_half[:, :], ALU.pow).then_inc(ro_pow, 1)

            two_spans(0)
            with pool.Fori(1, SPANS // 2) as it:
                two_spans(it)

        @block.vector
        def _(dve):
            def layer_norm_stats(j, par):
                return nc.vector.bn_stats(stats[:, j, :], xs[:, par, j, :])

            def layer_norm_apply(j, par):
                return nc.vector.tensor_scalar(xn[:, j, :], xs[:, par, j, :], mv[:, j, 0:1], rstd[:, j:j + 1],
                                               ALU.subtract, ALU.mult)

            def low_xt(j, bank):
                nc.vector.tensor_tensor(xt_lo[:, :, j * P:(j + 1) * P], D[bank][:, :].rearrange("p (k n) -> p k n", k=KT_),
                                        xt_hi[:, :, j * P:(j + 1) * P], ALU.subtract).then_inc(xt_lo_ready, 1)

            done = [0]

            def one(ins):
                ins.then_inc(set_v, 1)
                done[0] += 1
                dve.wait_ge(set_v, done[0])

            dve.wait_ge(x_loaded, 32)
            for j in range(TILES):
                one(layer_norm_stats(j, 0))
            for j in range(TILES):
                one(nc.vector.bn_aggr(mv[:, j, :], stats[:, j, :]))
            nc.vector.tensor_scalar(var_e[:, :], mv[:, :, 1], LN_EPS, None, ALU.add).then_inc(var_ready, 1)
            dve.wait_ge(rstd_ready, 1)
            for j in range(TILES):
                layer_norm_apply(j, 0).then_inc(xn_ready, 1)
            for j in range(TILES):
                dve.wait_ge(xt_hi_ready, j + 1)
                low_xt(j, XT_BANKS[j])

            flat = lambda t: t[:, :, :].rearrange("p n d -> p (n d)")
            one(nc.vector.memset(w_hi[:, :, 3 * DM:], 0.0))
            one(nc.vector.memset(w_lo[:, :, 3 * DM:], 0.0))
            dve.wait_ge(small_loaded, 16 * 7)
            dve.wait_ge(w_loaded[4], 16)
            one(nc.vector.tensor_scalar(flat(pt), flat(pt), onw4[:, :], None, ALU.mult))
            for n, src in enumerate((flat(qt), flat(kt), flat(vt), wb_raw[:, :, :].rearrange("p k c -> p (k c)"), flat(pt))):
                dve.wait_ge(w_loaded[n], 16)
                nc.vector.tensor_reduce(amax[:, n:n + 1], src, AX, ALU.max, apply_absolute_value=True).then_inc(amax_ready, 1)
            dve.wait_ge(amax_summed, 1)
            one(nc.vector.tensor_scalar(amax_all[:, :], amax_all[:, :], 2.0 ** -100, None, ALU.max))
            one(nc.vector.tensor_scalar(amax_e[:, :].bitcast(I32), amax_all[:, :].bitcast(I32), 0x7F800000, None, ALU.bitwise_and))
            one(nc.vector.tensor_scalar(w_scale[:, :].bitcast(I32), amax_e[:, :].bitcast(I32), -1.0, float((254 + 13) << 23),
                                        ALU.mult, ALU.add))
            one(nc.vector.tensor_scalar(w_inv[:, :].bitcast(I32), amax_e[:, :].bitcast(I32), float(13 << 23), None, ALU.subtract))
            nc.vector.tensor_scalar(w_inv[:, 3:4], w_inv[:, 3:4], 0.5, None, ALU.mult).then_inc(scales_ready, 1)
            wb_out = lambda w: w[:, :, 3 * DM:].rearrange("p k (h q) -> p k h q", q=32)[:, :, :, 0:MS]
            wb_in = wb_raw[:, :, :].rearrange("p k (m h) -> p k h m", h=QUADS)
            for k in range(KT_):
                one(nc.vector.tensor_scalar(wb_out(w_hi)[:, k], wb_in[:, k], w_scale[:, 3:4], None, ALU.mult))
            for k in range(KT_):
                ins = nc.vector.scalar_tensor_tensor(wb_out(w_lo)[:, k], wb_in[:, k], w_scale[:, 3:4], wb_out(w_hi)[:, k],
                                                     ALU.mult, ALU.subtract)
            ins.then_inc(proj_ready, 1)
            for n, src in enumerate((qt, kt, vt)):
                dve.wait_ge(hi_ready, n + 1)
                nc.vector.scalar_tensor_tensor(w_lo[:, :, n * DM:(n + 1) * DM],
                                               flat(src).rearrange("p (k c) -> p k c", k=KT_), w_scale[:, n:n + 1],
                                               w_hi[:, :, n * DM:(n + 1) * DM], ALU.mult, ALU.subtract).then_inc(proj_ready, 1)
            dve.wait_ge(hi_ready, 4)
            nc.vector.scalar_tensor_tensor(wo_lo[:, :, :], flat(pt).rearrange("p (k c) -> p k c", k=KT_), w_scale[:, 4:5],
                                           wo_hi[:, :, :], ALU.mult, ALU.subtract).then_inc(proj_ready, 1)
            dve.wait_ge(proj_ready, 5)

            def round_piece(n):
                w, c = raw[n % 2], magic[n % 2]
                dve.wait_ge(stage_loaded[n % 2], 16 * (n // 2 + 1))
                one(nc.vector.tensor_scalar(c.bitcast(I32), w.bitcast(I32), 0x7F800000, None, ALU.bitwise_and))
                one(nc.vector.tensor_scalar(c, c, 2.0 ** -6, 1.5 * 2.0 ** 20, ALU.max, ALU.mult))
                one(nc.vector.tensor_tensor(w, w, c, ALU.add))
                return w, c

            for n in range(8):
                w, c = round_piece(n)
                nc.vector.tensor_tensor(wgu[:, n // 2, (n % 2) * INNER:(n % 2 + 1) * INNER], w, c, ALU.subtract).then_inc(wgu_ready, 1)
                dve.wait_ge(wgu_ready, n + 1)
            dve.wait_ge(norms_full, 1)
            one(nc.vector.tensor_copy(bound[:, :], F[0][:, 0:2 * IC]))
            one(nc.vector.tensor_tensor(b_a[:, :], bound[:, 0:IC], bound[:, IC:], ALU.mult))
            for s in (gs, gs, us, us):
                one(nc.vector.tensor_tensor(b_a[:, :], b_a[:, :], s[:, :], ALU.mult))
            nc.vector.tensor_scalar(b_a[:, :], b_a[:, :], float(DM) ** 2, None, ALU.mult).then_inc(bound2_ready, 1)
            dve.wait_ge(bound_ready, 1)
            one(nc.vector.tensor_scalar(b_b[:, :], b_b[:, :], 2.0 ** -60, 2.0 ** 100, ALU.max, ALU.min))
            one(nc.vector.tensor_scalar(b_a[:, :].bitcast(I32), b_b[:, :].bitcast(I32), 0x7F800000, None, ALU.bitwise_and))
            one(nc.vector.tensor_scalar(row_fs[:, :].bitcast(I32), b_a[:, :].bitcast(I32), -1.0, float((254 + 14) << 23), ALU.mult, ALU.add))
            one(nc.vector.tensor_scalar(row_inv[:, :].bitcast(I32), b_a[:, :].bitcast(I32), float(14 << 23), None, ALU.subtract))
            one(nc.vector.tensor_tensor(usf[:, :], us[:, :], row_fs[:, :], ALU.mult))
            for n in range(8, 12):
                w, c = round_piece(n)
                one(nc.vector.tensor_tensor(w, w, c, ALU.subtract))
                for i in range(3):
                    ic = 3 * (n - 8) + i
                    ins = nc.vector.tensor_scalar(wd[:, ic, :], w[:, i * DM:(i + 1) * DM], row_inv[:, ic:ic + 1], None, ALU.mult)
                ins.then_inc(wd_ready, 1)
                dve.wait_ge(wd_ready, n - 7)
            one(nc.vector.memset(state[:, 0], 0.0))
            one(nc.vector.memset(mt[:, :], 0.0))
            dve.wait_ge(consts, 3 + QUADS)
            nc.vector.memset(xs[:, 1], 0.0).then_inc(ffn_ready, 1)
            dve.wait_ge(ffn_ready, 1)

            def two_spans(it):
                for par in range(2):
                    def since(per_span, n=0):
                        return at_span(it, par, per_span, n)

                    steps = [0]

                    def step(ins):
                        ins.then_inc(v_step, 1)
                        steps[0] += 1
                        return steps[0]

                    def after(n):
                        dve.wait_ge(v_step, since(V_STEPS, n))

                    def full(job):
                        dve.wait_ge(dense_done, since(DENSE, XT_FIRST + done_dense(job) + 1))
                        return job % 4

                    def group(t, m):
                        return flat(t)[:, m * TOK:(m + 1) * TOK]

                    def to_tokens(job, dst, ready):
                        bank = full(job)
                        nc.vector.transpose(dst, D[bank][:, :]).then_inc(ready, 1)

                    per_token = lambda s: s[:, :].unsqueeze(2).to_broadcast([P, MS * BC, DH])

                    for m in range(MS):
                        to_tokens(JOB_B + m, group(kt, m), k_raw)
                    for m in range(MS):
                        to_tokens(JOB_B + 4 + m, group(qt, m), q_raw)
                    to_tokens(JOB_B + 8, bt[:, :, :].rearrange("p c q -> p (c q)"), b_raw)
                    dve.wait_ge(k_sq, since(1, 1))
                    n = step(nc.vector.tensor_reduce(ssk[:, :], at[:, :].rearrange("p (n d) -> p n d", d=DH), AX, ALU.add))
                    after(n)
                    nc.vector.tensor_scalar(ssk[:, :], ssk[:, :], 1e-24, None, ALU.max).then_inc(ssk_ready, 1)
                    to_tokens(JOB_B + 9, group(vt, 0), v_raw)
                    dve.wait_ge(rk_pow, since(1, 1))
                    nc.vector.tensor_scalar(rk[:, :], rk[:, :], w_inv[:, 1:2], None, ALU.mult).then_inc(rk_ready, 1)
                    dve.wait_ge(q_sq, since(1, 1))
                    n = step(nc.vector.tensor_reduce(ssq[:, :], pt[:, :, :], AX, ALU.add))
                    after(n)
                    nc.vector.tensor_scalar(ssq[:, :], ssq[:, :], 1e-24, None, ALU.max).then_inc(ssq_ready, 1)
                    for m in range(1, MS):
                        to_tokens(JOB_B + 9 + m, group(vt, m), v_raw)
                    dve.wait_ge(tb_ready, since(1, 1))
                    step(nc.vector.tensor_scalar(beta[:, :], tb[:, :, :].rearrange("p m c -> p (m c)"), 0.5, 0.5, ALU.mult, ALU.add))
                    dve.wait_ge(rq_pow, since(1, 1))
                    n = step(nc.vector.tensor_scalar(rq[:, :], rq[:, :], w_inv[:, 0:1], float(DH) ** -0.5, ALU.mult, ALU.mult))
                    after(n)
                    q_done = step(nc.vector.tensor_tensor(qt[:, :, :], qt[:, :, :], per_token(rq), ALU.mult))
                    dve.wait_ge(acc_ready, since(TILES, 0))
                    for j in range(TILES):
                        bank = full(JOB_WO + j)
                        y = xs[:, 1 - par, j, :]
                        nc.vector.scalar_tensor_tensor(y, D[bank][:, :], w_inv[:, 4:5], y, ALU.mult, ALU.add).then_inc(wo_added, 1)

                    def fuse_tile(ic):
                        bank = full(JOB_GU + 2 * ic + 1)
                        dve.wait_ge(sg_ready, since(IC, ic + 1))
                        dve.wait_ge(flo_ready, since(IC, max(0, ic - 1)))
                        nc.vector.scalar_tensor_tensor(fuse[:, ic % 2, :], D[bank][:, :], usf[:, ic:ic + 1], sg[:, ic % 2, :],
                                                       ALU.mult, ALU.mult).then_inc(f_ready, 1)

                    def to_width(m):
                        for side, src in ((0, kt), (1, qt)):
                            ins = nc.vector.transpose(kq[:, m * BC:(m + 1) * BC, side, :], group(src, m).rearrange("p (n d) -> p n d", d=DH))
                            if side:
                                ins.then_inc(kq_ready, 1)

                    def read_gram(g):
                        dve.wait_ge(tiled_done, since(TILED, g + 1))
                        both = E[g % 2][:, :].rearrange("p (n a t) -> p n a t", n=8, a=2)
                        n0 = 8 * (g % 4)
                        step(nc.vector.tensor_tensor(a_nat[:, g // 4, n0:n0 + 8, :], both[:, :, 0, :],
                                                     beta[:, 8 * g:8 * g + 8].unsqueeze(2).to_broadcast([P, 8, CHUNK]), ALU.mult))
                        nc.vector.tensor_tensor(pt[:, 8 * g:8 * g + 8, :], both[:, :, 1, :],
                                                causal[:, :].unsqueeze(1).to_broadcast([P, 8, CHUNK]), ALU.mult).then_inc(p_ready, 1)

                    def by_problem(s):
                        after(steps[0])
                        nc.vector.transpose(m_prob[:, s], a_nat[:, s].rearrange("p n j -> p j n")).then_inc(m_ready, 1)

                    def solve_steps(j0, j1):
                        T, M = t_prob[:, 1], m_prob[:, 1]
                        for j in range(j0, j1):
                            rows, cols = CHUNK - 1 - j, j + 1
                            tmp = outer_v[:, 0:rows * cols].rearrange("p (i c) -> p i c", c=cols)
                            after(steps[0])
                            n = step(nc.vector.tensor_tensor(tmp, M[:, j, j + 1:].unsqueeze(2).to_broadcast([P, rows, cols]),
                                                             T[:, j, 0:cols].unsqueeze(1).to_broadcast([P, rows, cols]), ALU.mult))
                            after(n)
                            step(nc.vector.tensor_tensor(T[:, j + 1:, 0:cols], T[:, j + 1:, 0:cols], tmp, ALU.subtract))

                    def t_transposed(s):
                        n = step(nc.vector.transpose(tt[:, 32 * s:32 * s + 32, :].rearrange("p n t -> p t n"), t_prob[:, s]))
                        after(n)
                        nc.vector.tensor_tensor(tt[:, 32 * s:32 * s + 32, :], tt[:, 32 * s:32 * s + 32, :],
                                                beta[:, 32 * s:32 * s + 32].unsqueeze(2).to_broadcast([P, 32, CHUNK]),
                                                ALU.mult).then_inc(tt_ready, 1)

                    fuse_tile(0)
                    dve.wait_ge(kn_ready, since(1, 1))
                    after(q_done)
                    to_width(0)
                    to_width(1)
                    fuse_tile(1)
                    to_width(2)
                    to_width(3)
                    for ic in range(2, 6):
                        fuse_tile(ic)
                        read_gram(2 * (ic - 2))
                        read_gram(2 * (ic - 2) + 1)
                        if ic == 3:
                            by_problem(0)
                    fuse_tile(6)
                    by_problem(1)
                    dve.wait_ge(m_ready, since(2, 2))
                    n = step(nc.vector.memset(at[:, 1024:2048], 0.0))
                    after(n)
                    step(nc.vector.memset(at[:, 1024:2048:CHUNK + 1], 1.0))
                    solve_steps(0, 5)
                    for ic in range(7, IC):
                        fuse_tile(ic)
                        solve_steps(5 * (ic - 6), 5 * (ic - 5))
                    solve_steps(30, 31)
                    dve.wait_ge(t0_ready, since(1, 1))
                    t_transposed(0)
                    after(steps[0])
                    t_transposed(1)

                    for m in range(MS):
                        dve.wait_ge(tiled_done, since(TILED, DONE_UW + 2 * m + 1))
                        nc.vector.tensor_copy(group(vt, m), E[0][:, :]).then_inc(u_ready, 1)

                    def read_down(j):
                        bank = full(JOB_DN + j)
                        if j == 0:
                            dve.wait_ge(flo_ready, since(IC, IC))
                        dve.wait_ge(acc_ready, since(TILES, max(0, j - 1)))
                        nc.vector.tensor_tensor(fuse[:, j % 2, :], D[bank][:, :], ds_row[:, :], ALU.mult).then_inc(dn_ready, 1)

                    for c in range(STEPS):
                        dve.wait_ge(tiled_done, since(TILED, DONE_CHAIN + 3 * c + 1))
                        u = u_v[:, :, c]
                        nc.vector.tensor_tensor(u, u, E[0][:, 0:256].rearrange("p (b m d) -> p b m d", b=BATCH, m=MS),
                                                ALU.subtract).then_inc(r_ready, 1)
                        if c == 0:
                            dve.wait_ge(x_loaded, since(32, 64))
                            dve.nop(nofuse=True)
                            step(layer_norm_stats(0, 1 - par))
                            step(layer_norm_stats(1, 1 - par))
                        elif c == 1:
                            step(layer_norm_stats(2, 1 - par))
                            step(layer_norm_stats(3, 1 - par))
                        elif c == 2:
                            after(steps[0])
                            dve.nop(nofuse=True)
                            for j in range(TILES):
                                step(nc.vector.bn_aggr(mv[:, j, :], stats[:, j, :]))
                            after(steps[0])
                            nc.vector.tensor_scalar(var_e[:, :], mv[:, :, 1], LN_EPS, None, ALU.add).then_inc(var_ready, 1)
                        elif c in (3, 4):
                            dve.wait_ge(rstd_ready, since(1, 2))
                            for j in (2 * c - 6, 2 * c - 5):
                                layer_norm_apply(j, 1 - par).then_inc(xn_ready, 1)
                        dve.wait_ge(tiled_done, since(TILED, DONE_CHAIN + 3 * c + 2))
                        s_flat = lambda k: state[:, k].rearrange("p b m d -> p (b m d)")
                        dve.wait_ge(s_ready, since(STEPS, c))
                        nc.vector.tensor_tensor(s_flat(1 - c % 2), s_flat(c % 2), E[1][:, 0:256], ALU.add).then_inc(s_ready, 1)
                        if c in (2, 4, 6):
                            read_down(c // 2 - 1)
                        if c == STEPS - 2:
                            for j in range(TILES):
                                dve.wait_ge(xt_hi_ready, since(TILES, TILES + j + 1))
                                low_xt(j, XT_BANKS[j])
                    read_down(3)
                    dve.wait_ge(o_sq, since(1, 1))
                    n = step(nc.vector.tensor_reduce(sso[:, :], pt[:, :, :], AX, ALU.add))
                    after(n)
                    nc.vector.tensor_scalar(sso[:, :], sso[:, :], 1.0 / DH, O_EPS, ALU.mult, ALU.add).then_inc(sso_ready, 1)
                    dve.wait_ge(ro_pow, since(1, 1))
                    n = step(nc.vector.tensor_tensor(qt[:, :, :], qt[:, :, :], per_token(ro), ALU.mult))
                    after(n)
                    nc.vector.transpose(kq_flat[:, 0:2048], flat(qt)).then_inc(ot_ready, 1)
                    dve.wait_ge(ohi_ready, since(1, 1))
                    nc.vector.tensor_tensor(o_split[:, 1], o_t, o_split[:, 0], ALU.subtract).then_inc(olo_ready, 1)
                    assert steps[0] == V_STEPS, steps

            two_spans(0)
            with dve.Fori(1, SPANS // 2) as it:
                two_spans(it)

            dve.wait_ge(acc_ready, TILES * SPANS)
            for j in range(TILES):
                dve.wait_ge(dense_done, XT_FIRST + SPANS * DENSE + j + 1)
                y = xs[:, 1, j, :]
                nc.vector.scalar_tensor_tensor(y, D[j][:, :], w_inv[:, 4:5], y, ALU.mult, ALU.add).then_inc(wo_added, 1)


_INS = ['L0_attn_hidden_states', 'L0_attn_Wq', 'L0_attn_Wk', 'L0_attn_Wv', 'L0_attn_Wb', 'L0_attn_o_norm_weight',
        'L0_attn_Wo', 'L0_ffn_gate_w', 'L0_ffn_up_w', 'L0_ffn_down_w', 'L0_ffn_gate_scale', 'L0_ffn_up_scale',
        'L0_ffn_down_scale']


def kernel(**inputs):
    import numpy as _np
    import concourse.bacc as _bacc
    from concourse import mybir as _mybir
    from concourse.bass_utils import run_bass_kernel_spmd as _run

    nc = _bacc.Bacc("TRN2", target_bir_lowering=False, num_devices=1)
    arrays, args = {}, []
    for name in _INS:
        a = _np.ascontiguousarray(inputs[name])
        arrays[f"in_{name}_dram"] = a
        args.append(nc.dram_tensor(f"in_{name}_dram", a.shape, _mybir.dt.from_np(a.dtype), kind="ExternalInput").ap())
    out = nc.dram_tensor("out_0_dram", (BATCH, LENGTH, DM), _mybir.dt.float32, kind="ExternalOutput").ap()
    delta_block_kernel(nc, *args, out)
    r = _run(nc, [arrays], core_ids=[0])
    return r.results[0]["out_0_dram"]
```

```python
import concourse.bass as bass
from concourse import mybir
from contextlib import ExitStack

BATCH, LENGTH, DM = 2, 4096, 512
HEADS, DH = 16, 32
INNER = 1536
P = 128
SPAN_B = 256
SPANS = LENGTH // SPAN_B
TOK = BATCH * SPAN_B
TILES = TOK // P
CHUNK = 32
STEPS = SPAN_B // CHUNK
BC = BATCH * STEPS
QUADS = P // DH
MS = HEADS // QUADS
KT_ = DM // P
IC = INNER // P
LN_EPS = O_EPS = 1e-05

JOB_K, JOB_V, JOB_B, JOB_Q, JOB_WO, JOB_DN = 0, 4, 8, 9, 21, 41
PROJECTIONS = 13
XT_BANKS = [1, 2, 3, 1]
DENSE, XT_FIRST = 49, 4
DONE_XT = 44
TILED = 32
DONE_UW, DONE_CHAIN = 8, 16
V_STEPS, P_STEPS = 160, 100
FUSE_RING = 4
SPLIT = 11
LOW_FIRST = 4
LOW_AT = {18: 1, 30: 2}
LEAD = 15
OUT_AT = {17: 0, 19: 1, 21: 2, 24: 3}
FUSE_AT = {15: 3, 25: 4, 28: 5, 31: 6, 34: 7}
W_AT = {35: 0, 38: 1, 41: 2}
NEWTONS = 3


def gate_up_job(half):
    return 13 + half if half < 8 else 17 + half


def done_dense(job):
    return job if job < JOB_DN + 3 else DENSE - 1


def delta_block_kernel(nc: bass.Bass, x: bass.AP, wq: bass.AP, wk: bass.AP, wv: bass.AP, wb: bass.AP,
                       onw: bass.AP, wo: bass.AP, gate_w: bass.AP, up_w: bass.AP, down_w: bass.AP,
                       gate_s: bass.AP, up_s: bass.AP, down_s: bass.AP, out: bass.AP):
    F32, F16, BF16, I32 = mybir.dt.float32, mybir.dt.float16, mybir.dt.bfloat16, mybir.dt.int32
    ALU = mybir.AluOpType
    ACT = mybir.ActivationFunctionType
    AX = mybir.AxisListType.X

    x_v = x.rearrange("b (i h p) d -> b i p h d", h=2, p=P)
    out_v = out.rearrange("b (i h p) d -> b i p h d", h=2, p=P)

    ctx = ExitStack()
    with ctx:
        def sb(name, shape, dt=F32):
            return ctx.enter_context(nc.sbuf_tensor(name, shape, dt))

        def sem(name):
            return ctx.enter_context(nc.semaphore(name))

        w_hi = sb("w_hi", [P, KT_, 3 * DM + P], F16)
        w_lo = sb("w_lo", [P, KT_, 3 * DM + P], F16)
        wo_hi = sb("wo_hi", [P, MS, DM], F16)
        wo_lo = sb("wo_lo", [P, MS, DM], F16)
        wgu = sb("wgu", [P, KT_, 2 * INNER], F16)
        wd = sb("wd", [P, IC, DM], BF16)
        xs = sb("xs", [P, 2, TILES, DM])
        xt_hi = sb("xt_hi", [P, KT_, TOK], F16)
        xt_lo = sb("xt_lo", [P, KT_, TOK], F16)
        f_hi = sb("f_hi", [P, IC, TOK], F16)
        f_lo = sb("f_lo", [P, IC, TOK], F16)
        sg = sb("sg", [P, 2, TOK])
        fuse = sb("fuse", [P, FUSE_RING, TOK])
        kpv = sb("kpv", [P, 3, MS * BC * DH])
        qt = sb("qt", [P, MS * BC, DH])
        kq = sb("kq", [P, MS * BC, 2, CHUNK])
        at = sb("at", [P, 2048])
        mt = sb("mt", [P, 2048])
        outer_v = sb("outer_v", [P, 512])
        outer_p = sb("outer_p", [P, 256])
        state = sb("state", [P, BATCH, MS, DH])
        bt = sb("bt", [P, BC, CHUNK])
        tb = sb("tb", [P, MS, BC])
        beta = sb("beta", [P, MS * BC])
        ssk, ssq, sso = (sb(n, [P, MS * BC]) for n in ("ssk", "ssq", "sso"))
        rk, ro, newton = (sb(n, [P, MS * BC]) for n in ("rk", "ro", "newton"))
        q_scale = sb("q_scale", [P, 1])
        stats = sb("stats", [P, TILES, 6])
        mv = sb("mv", [P, TILES, 2])
        var_e = sb("var_e", [P, TILES])
        rstd = sb("rstd", [P, TILES])
        ident = sb("ident", [P, P])
        causal = sb("causal", [P, CHUNK])
        ones = sb("ones", [P, 1])
        neg_half = sb("neg_half", [P, MS * BC])
        pos_half = sb("pos_half", [P, IC])
        gs = sb("gs", [P, IC])
        us = sb("us", [P, IC])
        usf = sb("usf", [P, IC])
        row_inv = sb("row_inv", [P, IC])
        row_fs = sb("row_fs", [P, IC])
        bound = sb("bound", [P, 2 * IC])
        b_a = sb("b_a", [P, IC])
        b_b = sb("b_b", [P, IC])
        ds_row = sb("ds_row", [P, DM])
        onw4 = sb("onw4", [P, 1])
        wb_raw = sb("wb_raw", [P, KT_, HEADS])
        amax = sb("amax", [P, 5])
        amax_all = sb("amax_all", [P, 5])
        amax_e = sb("amax_e", [P, 5])
        w_scale = sb("w_scale", [P, 5])
        w_inv = sb("w_inv", [P, 5])

        D = [ctx.enter_context(nc.psum_tensor(f"D{b}", [P, 512], F32)) for b in range(4)]
        T = [ctx.enter_context(nc.psum_tensor(f"T{b}", [P, 512], F32)) for b in range(4)]

        kt, pt, vt = (kpv[:, i, :].rearrange("p (n d) -> p n d", d=DH) for i in range(3))
        t_flat = qt[:, :, :].rearrange("p n d -> p (n d)")
        a_nat = at[:, :].rearrange("p (g n s) -> p g n s", g=2, n=32)
        t_prob = t_flat.rearrange("p (g i c) -> p g i c", g=2, i=CHUNK)
        m_prob = mt[:, :].rearrange("p (g j i) -> p g j i", g=2, j=CHUNK)
        tt = mt[:, :].rearrange("p (n t) -> p n t", t=CHUNK)
        xn = at[:, :].rearrange("p (j d) -> p j d", j=TILES)
        o_hi, o_lo = f_hi[:, IC - MS:, :], f_lo[:, IC - MS:, :]
        kq_flat = kq[:, :, :, :].rearrange("p n a t -> p (n a t)")
        o_t = kq_flat[:, 0:2048].rearrange("p (m n) -> p m n", m=MS)
        o_tok = kq_flat[:, 2048:4096]
        u_v = vt[:, :, :].rearrange("p (m b c) d -> p b c m d", m=MS, b=BATCH)
        ot_v = qt[:, :, :].rearrange("p (m b c) t -> p b c m t", m=MS, b=BATCH)
        sq_acc = f_hi[:, :, :].rearrange("p a b -> p (a b)").bitcast(F32)
        raw = [kq_flat[:, 0:INNER], kq_flat[:, INNER:2 * INNER]]
        magic = [at[:, 0:INNER], mt[:, 0:INNER]]
        vt_flat = vt[:, :, :].rearrange("p n d -> p (n d)")

        dense_done, tiled_done = sem("dense_done"), sem("tiled_done")
        x_loaded, y_stored = sem("x_loaded"), sem("y_stored")
        w_loaded = [sem(f"w_loaded{n}") for n in range(5)]
        small_loaded = sem("small_loaded")
        stage_loaded = [sem(f"stage_loaded{n}") for n in range(2)]
        wd_ready = sem("wd_ready")
        consts = sem("consts")
        amax_ready, amax_summed, scales_ready = sem("amax_ready"), sem("amax_summed"), sem("scales_ready")
        hi_ready, proj_ready = sem("hi_ready"), sem("proj_ready")
        wgu_ready, sq_ready, sq_added = sem("wgu_ready"), sem("sq_ready"), sem("sq_added")
        norms_full, bound2_ready, bound_ready, ffn_ready = (
            sem("norms_full"), sem("bound2_ready"), sem("bound_ready"), sem("ffn_ready"))
        set_v = sem("set_v")
        var_ready, rstd_ready, xn_ready = sem("var_ready"), sem("rstd_ready"), sem("xn_ready")
        xt_hi_ready, xt_lo_ready = sem("xt_hi_ready"), sem("xt_lo_ready")
        k_raw, q_raw, v_raw, b_raw = sem("k_raw"), sem("q_raw"), sem("v_raw"), sem("b_raw")
        k_sq, q_sq, tb_ready, v_ready = sem("k_sq"), sem("q_sq"), sem("tb_ready"), sem("v_ready")
        ssk_ready, rk_ready, kq_ready = sem("ssk_ready"), sem("rk_ready"), sem("kq_ready")
        m_ready, zero_ready, diag_ready, t_ready = sem("m_ready"), sem("zero_ready"), sem("diag_ready"), sem("t_ready")
        tt_ready, p_ready = sem("tt_ready"), sem("p_ready")
        u_ready, w_ready, r_ready, s_ready = sem("u_ready"), sem("w_ready"), sem("r_ready"), sem("s_ready")
        ws_read, qs_ready, otok_ready = sem("ws_read"), sem("qs_ready"), sem("otok_ready")
        sg_ready, f_ready, fhi_ready, flo_ready = sem("sg_ready"), sem("f_ready"), sem("fhi_ready"), sem("flo_ready")
        dn_ready, acc_ready, wo_added = sem("dn_ready"), sem("acc_ready"), sem("wo_added")
        o_ready, o_sq, sso_ready, ro_ready = sem("o_ready"), sem("o_sq"), sem("sso_ready"), sem("ro_ready")
        ot_ready, ohi_ready, olo_ready = sem("ot_ready"), sem("ohi_ready"), sem("olo_ready")
        v_step, p_step = sem("v_step"), sem("p_step")

        def at_span(it, par, per_span, n=0):
            return it * (2 * per_span) + (par * per_span + n)

        block = ctx.enter_context(nc.Block())

        @block.sync
        def _(sp):
            for b in range(BATCH):
                sp.dma_start(xs[:, 0, 2 * b:2 * b + 2, :], x_v[b, 0]).then_inc(x_loaded, 16)
            for n, (dst, src) in enumerate(((qt, wq), (kt, wk), (vt, wv))):
                sp.dma_start(dst[:, :, :].rearrange("p n d -> p (n d)").rearrange("p (k c) -> p k c", k=KT_),
                             src.rearrange("(k p) c -> p k c", p=P)).then_inc(w_loaded[n], 16)
            sp.dma_start(wb_raw[:, :, :], wb.rearrange("(k p) c -> p k c", p=P)).then_inc(w_loaded[3], 16)
            sp.dma_start(pt[:, :, :].rearrange("p n d -> p (n d)").rearrange("p (k c) -> p k c", k=KT_),
                         wo.rearrange("(k p) c -> p k c", p=P)).then_inc(w_loaded[4], 16)
            for h in range(QUADS):
                sp.dma_start(onw4[32 * h:32 * h + 32, :], onw.rearrange("(d o) -> d o", o=1), allow_slow_non_contiguous=True).then_inc(small_loaded, 16)
            sp.dma_start(gs[:, :], gate_s.rearrange("(c p) -> p c", p=P), allow_slow_non_contiguous=True).then_inc(small_loaded, 16)
            sp.dma_start(us[:, :], up_s.rearrange("(c p) -> p c", p=P), allow_slow_non_contiguous=True).then_inc(small_loaded, 16)
            sp.dma_start(ds_row[:, :], down_s.partition_broadcast(P)).then_inc(small_loaded, 16)
            for n in range(12):
                if n >= 2:
                    if n - 2 < 8:
                        sp.wait_ge(wgu_ready, n - 1)
                    else:
                        sp.wait_ge(wd_ready, n - 9)
                if n < 8:
                    src = (gate_w, up_w)[n % 2][(n // 2) * P:(n // 2 + 1) * P, :]
                    sp.dma_start(raw[n % 2], src).then_inc(stage_loaded[n % 2], 16)
                else:
                    r = 3 * (n - 8) * P
                    sp.dma_start(raw[n % 2].rearrange("p (c d) -> p c d", c=3),
                                 down_w[r:r + 3 * P, :].rearrange("(c p) d -> p c d", p=P)).then_inc(stage_loaded[n % 2], 16)

            def load_x(span, par):
                for b in range(BATCH):
                    sp.dma_start(xs[:, par, 2 * b:2 * b + 2, :], x_v[b, span]).then_inc(x_loaded, 16)

            def store_y(span, par):
                for b in range(BATCH):
                    sp.dma_start(out_v[b, span], xs[:, par, 2 * b:2 * b + 2, :]).then_inc(y_stored, 16)

            sp.wait_ge(wo_added, TILES)
            load_x(1, 1)
            with sp.Fori(0, (SPANS - 2) // 2) as it:
                for par in range(2):
                    sp.wait_ge(wo_added, at_span(it, par, TILES, 2 * TILES))
                    sp.nop(nofuse=True)
                    store_y(it * 2 + par, par)
                    sp.wait_ge(y_stored, at_span(it, par, 32, 32))
                    sp.nop(nofuse=True)
                    load_x(it * 2 + (par + 2), par)
            sp.wait_ge(wo_added, TILES * SPANS)
            store_y(SPANS - 2, 0)
            sp.wait_ge(y_stored, 32 * (SPANS - 1))
            load_x(0, 0)
            sp.wait_ge(wo_added, TILES * (SPANS + 1))
            store_y(SPANS - 1, 1)
            sp.wait_ge(y_stored, 32 * SPANS)
            sp.wait_ge(x_loaded, 32 * (SPANS + 1))

        @block.tensor
        def _(pe):
            def quads(out, lhs, rhs, start=True, stop=True):
                for h in range(QUADS):
                    s = slice(32 * h, 32 * h + 32)
                    last = nc.tensor.matmul(out[s], lhs[s], rhs[s], start=start, stop=stop)
                return last

            def transpose_xn(j, bank):
                for k in range(KT_):
                    last = nc.tensor.transpose(D[bank][:, k * P:(k + 1) * P], xn[:, j, k * P:(k + 1) * P], ident[:, :])
                last.then_inc(dense_done, 1)

            def project_out(j, bank):
                n = 0
                for m in range(MS):
                    for o_part, w in ((o_hi, wo_hi), (o_lo, wo_hi), (o_hi, wo_lo)):
                        last = nc.tensor.matmul(D[bank][:, :], o_part[:, m, j * P:(j + 1) * P], w[:, m, :],
                                                start=n == 0, stop=n == 3 * MS - 1)
                        n += 1
                last.then_inc(dense_done, 1)

            pe.wait_ge(consts, 2)
            for j in range(TILES):
                b = XT_BANKS[j]
                pe.wait_ge(xn_ready, j + 1)
                if j == 3:
                    pe.wait_ge(xt_lo_ready, 1)
                transpose_xn(j, b)
            pe.wait_ge(sq_added, 8)
            for c in range(2 * IC):
                last = nc.tensor.matmul(T[0][:, c:c + 1], sq_acc[:, c * P:(c + 1) * P], ones[:, :], start=True, stop=True)
            last.then_inc(norms_full, 1)
            pe.wait_ge(proj_ready, 5)
            pe.wait_ge(ffn_ready, 1)

            def two_spans(it):
                for par in range(2):
                    def since(per_span, n=0):
                        return at_span(it, par, per_span, n)

                    def take(job):
                        before = job - 4
                        if before < 0:
                            pe.wait_ge(*((dn_ready, since(TILES)) if job == 0 else (xt_lo_ready, since(TILES, TILES))))
                        elif before < JOB_V:
                            pe.wait_ge(k_raw, since(MS, before + 1))
                        elif before < JOB_B:
                            pe.wait_ge(v_raw, since(MS, before - JOB_V + 1))
                        elif before < JOB_Q:
                            pe.wait_ge(b_raw, since(1, 1))
                        elif before < PROJECTIONS:
                            pe.wait_ge(q_raw, since(MS, before - JOB_Q + 1))
                        elif JOB_WO <= before < JOB_WO + TILES:
                            pe.wait_ge(wo_added, since(TILES, before - JOB_WO + 1))
                        else:
                            half = before - (PROJECTIONS if before < JOB_WO else PROJECTIONS + TILES)
                            pe.wait_ge(f_ready if half % 2 else sg_ready, since(IC, half // 2 + 1))
                        return job % 4

                    pe.wait_ge(xt_lo_ready, since(TILES, TILES))
                    for job in range(PROJECTIONS):
                        g = (4, 5, 6, 7, 8, 9, 10, 11, 12, 0, 1, 2, 3)[job]
                        bank = take(job)
                        cols = slice(g * P, (g + 1) * P)
                        n = 0
                        for k in range(KT_):
                            for w, xp in ((w_hi, xt_hi), (w_hi, xt_lo), (w_lo, xt_hi)):
                                last = nc.tensor.matmul(D[bank][:, :], w[:, k, cols], xp[:, k, :],
                                                        start=n == 0, stop=n == 3 * KT_ - 1)
                                n += 1
                        last.then_inc(dense_done, 1)

                    def gate_up(half):
                        bank = take(gate_up_job(half))
                        ic, side = divmod(half, 2)
                        c = side * INNER + ic * P
                        for k in range(KT_):
                            nc.tensor.matmul(D[bank][:, :], wgu[:, k, c:c + P], xt_hi[:, k, :], start=k == 0, stop=False)
                            last = nc.tensor.matmul(D[bank][:, :], wgu[:, k, c:c + P], xt_lo[:, k, :],
                                                    start=False, stop=k == KT_ - 1)
                        last.then_inc(dense_done, 1)

                    def gram(g):
                        pe.wait_ge(kq_ready, since(MS, g // 2 + 1))
                        if g < 4:
                            pe.wait_ge(qs_ready if g < 2 else o_ready, since(STEPS))
                        else:
                            pe.wait_ge(p_ready, since(8, g - 3))
                        pe.nop(nofuse=True)
                        for n in range(8):
                            both = kq_flat.rearrange("p (n t) -> p n t", t=2 * CHUNK)[:, 8 * g + n, :]
                            last = quads(T[g % 4][:, 64 * n:64 * n + 64], both[:, 0:CHUNK], both)
                        last.then_inc(tiled_done, 1)

                    for g in range(8):
                        gram(g)
                        gate_up(g)
                    pe.wait_ge(olo_ready, since(1, 1))
                    for j in range(TILES):
                        project_out(j, take(JOB_WO + j))
                    for half in range(8, 16):
                        gate_up(half)

                    pe.wait_ge(v_ready, since(1, 1))
                    for g in range(8):
                        pe.wait_ge(tt_ready, since(2, g // 4 + 1))
                        pe.wait_ge(*((u_ready, since(8, g - 3)) if g >= 4 else (p_ready, since(8, g + 5))))
                        pe.nop(nofuse=True)
                        for n in range(8):
                            pc = 8 * g + n
                            last = quads(T[g % 4][:, 64 * n:64 * n + 64], tt[:, pc, :], kpv[:, 0:3:2, pc * DH:(pc + 1) * DH])
                        last.then_inc(tiled_done, 1)
                        gate_up(16 + g)

                    def down(j, part):
                        bank = (JOB_DN + j) % 4
                        if j == 0:
                            pe.wait_ge(flo_ready, since(IC, 3 * part + 3))
                        for ic in range(3 * part, 3 * part + 3):
                            nc.tensor.matmul(D[bank][:, :], f_hi[:, ic, j * P:(j + 1) * P], wd[:, ic, :], start=ic == 0, stop=False)
                            last = nc.tensor.matmul(D[bank][:, :], f_lo[:, ic, j * P:(j + 1) * P], wd[:, ic, :],
                                                    start=False, stop=ic == IC - 1)
                        if part == 3:
                            last.then_inc(dense_done, 1)

                    for c in range(STEPS):
                        if c == 0:
                            pe.wait_ge(w_ready, since(8, 8))
                        pe.wait_ge(s_ready, since(STEPS, c))
                        pe.wait_ge(*((qs_ready, since(STEPS, c - 1)) if c >= 2 else (u_ready, since(8, 8))))
                        pe.nop(nofuse=True)
                        for b in range(BATCH):
                            for m in range(MS):
                                n, pc = b * MS + m, m * BC + b * STEPS + c
                                last = quads(T[c % 2][:, 64 * n:64 * n + 64], state[:, b, m, :],
                                             kq_flat[:, 64 * pc:64 * pc + 64])
                        last.then_inc(tiled_done, 1)
                        if c % 2 == 0:
                            take(JOB_DN + c // 2)
                        down(c // 2, 2 * (c % 2))
                        pe.wait_ge(r_ready, since(STEPS, c + 1))
                        if c >= 2:
                            pe.wait_ge(o_ready, since(STEPS, c - 1))
                        pe.nop(nofuse=True)
                        for b in range(BATCH):
                            for m in range(MS):
                                n, pc = b * MS + m, m * BC + b * STEPS + c
                                last = quads(T[2 + c % 2][:, 64 * n:64 * n + 64], vt[:, pc, :],
                                             kpv[:, 0:2, pc * DH:(pc + 1) * DH])
                        last.then_inc(tiled_done, 1)
                        down(c // 2, 2 * (c % 2) + 1)
                        if c == STEPS - 2:
                            for j in range(TILES):
                                pe.wait_ge(xn_ready, since(TILES, TILES + j + 1))
                                pe.wait_ge(*((dn_ready, since(TILES, j + 1)) if j < 3 else (xt_lo_ready, since(TILES, TILES + 1))))
                                transpose_xn(j, XT_BANKS[j])

            two_spans(0)
            with pe.Fori(1, SPANS // 2) as it:
                two_spans(it)

            pe.wait_ge(olo_ready, SPANS + 1)
            pe.wait_ge(dn_ready, TILES * SPANS)
            pe.wait_ge(xt_lo_ready, TILES * (SPANS + 1))
            for j in range(TILES):
                project_out(j, j)

        @block.scalar
        def _(act):
            def evacuate_xt(j, bank):
                nc.scalar.activation(xt_hi[:, :, j * P:(j + 1) * P], D[bank][:, :].rearrange("p (k n) -> p k n", k=KT_),
                                     ACT.Copy).then_inc(xt_hi_ready, 1)

            for j in range(TILES):
                act.wait_ge(dense_done, j + 1)
                evacuate_xt(j, XT_BANKS[j])
            act.wait_ge(scales_ready, 1)
            for n, src in enumerate((qt, kt, vt)):
                nc.scalar.activation(w_hi[:, :, n * DM:(n + 1) * DM],
                                     src[:, :, :].rearrange("p n d -> p (n d)").rearrange("p (k c) -> p k c", k=KT_),
                                     ACT.Identity, scale=w_scale[:, n:n + 1]).then_inc(hi_ready, 1)
            nc.scalar.activation(wo_hi[:, :, :], pt[:, :, :].rearrange("p n d -> p (n d)").rearrange("p (k c) -> p k c", k=KT_),
                                 ACT.Identity, scale=w_scale[:, 4:5]).then_inc(hi_ready, 1)
            act.wait_ge(proj_ready, 5)
            for n in range(8):
                act.wait_ge(wgu_ready, n + 1)
                if n >= 1:
                    act.wait_ge(sq_added, n)
                nc.scalar.activation(vt_flat[:, 0:INNER], wgu[:, n // 2, (n % 2) * INNER:(n % 2 + 1) * INNER],
                                     ACT.Square).then_inc(sq_ready, 1)
            act.wait_ge(ffn_ready, 1)
            flat = lambda t: t[:, :, :].rearrange("p n d -> p (n d)")

            def o_squares(it, par):
                act.wait_ge(otok_ready, at_span(it, par, 1, 1))
                nc.scalar.activation(flat(pt), o_tok, ACT.Square, scale=q_scale[:, :]).then_inc(o_sq, 1)

            def o_high(it, par):
                act.wait_ge(ot_ready, at_span(it, par, 1, 1))
                nc.scalar.activation(o_hi, o_t, ACT.Copy).then_inc(ohi_ready, 1)

            def two_spans(it):
                for par in range(2):
                    def since(per_span, n=0):
                        return at_span(it, par, per_span, n)

                    def full(job):
                        act.wait_ge(dense_done, since(DENSE, XT_FIRST + done_dense(job) + 1))
                        return job % 4

                    o_squares(it, par)
                    act.wait_ge(k_raw, since(MS, MS))
                    nc.scalar.activation(at[:, :], flat(kt), ACT.Square, scale=w_inv[:, 1:2]).then_inc(k_sq, 1)
                    o_high(it, par)
                    act.wait_ge(v_raw, since(MS, MS))
                    nc.scalar.activation(flat(vt), flat(vt), ACT.Silu, scale=w_inv[:, 2:3]).then_inc(v_ready, 1)
                    act.wait_ge(b_raw, since(1, 1))
                    nc.scalar.activation(tb[:, :, :], bt[:, :, 0:MS].rearrange("p c m -> p m c"), ACT.Tanh,
                                         scale=w_inv[:, 3:4]).then_inc(tb_ready, 1)
                    for m in range(MS):
                        act.wait_ge(q_raw, since(MS, m + 1))
                        nc.scalar.activation(flat(pt)[:, m * TOK:(m + 1) * TOK], flat(qt)[:, m * TOK:(m + 1) * TOK],
                                             ACT.Square, scale=w_inv[:, 0:1]).then_inc(q_sq, 1)

                    def high_part(ic):
                        act.wait_ge(f_ready, since(IC, ic + 1))
                        nc.scalar.activation(f_hi[:, ic, :], fuse[:, ic % FUSE_RING, :], ACT.Copy).then_inc(fhi_ready, 1)

                    def silu_gate(ic):
                        bank = full(gate_up_job(2 * ic))
                        nc.scalar.activation(sg[:, ic % 2, :], D[bank][:, :], ACT.Silu,
                                             scale=gs[:, ic:ic + 1]).then_inc(sg_ready, 1)
                        if ic % 8:
                            high_part(ic - 1)

                    def copy_u(g):
                        act.wait_ge(w_ready, since(8, g + 1))
                        nc.scalar.activation(vt[:, 8 * g:8 * g + 8, :],
                                             T[g % 4][:, :].rearrange("p (n a d) -> p n a d", n=8, a=2)[:, :, 1, :],
                                             ACT.Copy).then_inc(u_ready, 1)

                    for ic in range(8):
                        silu_gate(ic)
                    high_part(7)
                    for g in range(8):
                        copy_u(g)
                        if g % 2 == 0:
                            silu_gate(8 + g // 2)
                    high_part(IC - 1)
                    for c in range(STEPS):
                        act.wait_ge(ws_read, since(STEPS, c + 1))
                        nc.scalar.activation(ot_v[:, :, c], T[c % 2][:, :].rearrange("p (b m a t) -> p b m a t", b=BATCH, m=MS, a=2)[:, :, :, 1, :],
                                             ACT.Copy).then_inc(qs_ready, 1)
                        if c == STEPS - 2:
                            for j in range(TILES):
                                act.wait_ge(dense_done, since(DENSE, XT_FIRST + DONE_XT + j + 1))
                                evacuate_xt(j, XT_BANKS[j])

            two_spans(0)
            with act.Fori(1, SPANS // 2) as it:
                two_spans(it)
            o_squares(SPANS // 2, 0)
            o_high(SPANS // 2, 0)

        @block.gpsimd
        def _(pool):
            nc.gpsimd.memset(ident[:, :], 0.0).then_inc(consts, 1)
            pool.wait_ge(consts, 1)
            nc.gpsimd.affine_select(out=ident[:, :], in_=ident[:, :], compare_op=ALU.not_equal, fill=1.0, base=0,
                                    pattern=[[-1, P]], channel_multiplier=1).then_inc(consts, 1)
            nc.gpsimd.memset(neg_half[:, :], -0.5)
            nc.gpsimd.memset(pos_half[:, :], 0.5)
            nc.gpsimd.memset(ones[:, :], 1.0)
            nc.gpsimd.memset(sq_acc, 0.0)
            nc.gpsimd.memset(causal[:, :], 1.0).then_inc(consts, 1)
            pool.wait_ge(consts, 3)
            for h in range(QUADS):
                c = causal[32 * h:32 * h + 32, :]
                nc.gpsimd.affine_select(out=c, in_=c, compare_op=ALU.is_ge, fill=0.0, base=0,
                                        pattern=[[1, CHUNK]], channel_multiplier=-1).then_inc(consts, 1)
                pool.wait_ge(consts, 4 + h)
            pool.wait_ge(var_ready, 1)
            nc.gpsimd.tensor_tensor(rstd[:, :], var_e[:, :], neg_half[:, 0:TILES], ALU.pow).then_inc(rstd_ready, 1)
            pool.wait_ge(amax_ready, 5)
            nc.gpsimd.partition_all_reduce(amax_all[:, :], amax[:, :], P, bass.bass_isa.ReduceOp.absmax).then_inc(amax_summed, 1)
            for n in range(8):
                acc = sq_acc[:, (n % 2) * INNER:(n % 2 + 1) * INNER]
                pool.wait_ge(sq_ready, n + 1)
                if n:
                    pool.wait_ge(sq_added, n)
                nc.gpsimd.tensor_tensor(acc, acc, vt_flat[:, 0:INNER], ALU.add).then_inc(sq_added, 1)
            pool.wait_ge(bound2_ready, 1)
            nc.gpsimd.tensor_tensor(b_b[:, :], b_a[:, :], pos_half[:, :], ALU.pow).then_inc(bound_ready, 1)
            pool.wait_ge(ffn_ready, 1)

            def inverse_root(x, y, step, after_last):
                for n in range(NEWTONS):
                    if n:
                        after_last()
                    step(nc.gpsimd.tensor_tensor(newton[:, :], y, y, ALU.mult))
                    after_last()
                    step(nc.gpsimd.tensor_tensor(newton[:, :], newton[:, :], x, ALU.mult))
                    after_last()
                    step(nc.gpsimd.tensor_scalar(newton[:, :], newton[:, :], -0.5, 1.5, ALU.mult, ALU.add))
                    after_last()
                    last = nc.gpsimd.tensor_tensor(y, y, newton[:, :], ALU.mult)
                    if n < NEWTONS - 1:
                        step(last)
                return last

            def o_norm(it, par, step, after_last):
                pool.wait_ge(sso_ready, at_span(it, par, 1, 1))
                inverse_root(sso[:, :], ro[:, :], step, after_last).then_inc(ro_ready, 1)

            def o_low(it, par):
                pool.wait_ge(ohi_ready, at_span(it, par, 1, 1))
                nc.gpsimd.tensor_tensor(o_lo, o_t, o_hi, ALU.subtract).then_inc(olo_ready, 1)

            def two_spans(it):
                for par in range(2):
                    def since(per_span, n=0):
                        return at_span(it, par, per_span, n)

                    steps = [0]

                    def step(ins):
                        ins.then_inc(p_step, 1)
                        steps[0] += 1

                    def after_last():
                        pool.wait_ge(p_step, since(P_STEPS, steps[0]))
                        pool.nop(nofuse=True)

                    o_norm(it, par, step, after_last)
                    pool.wait_ge(ssk_ready, since(1, 1))
                    inverse_root(ssk[:, :], rk[:, :], step, after_last).then_inc(rk_ready, 1)
                    o_low(it, par)

                    def low_part(ic):
                        pool.wait_ge(fhi_ready, since(IC, ic + 1))
                        pool.nop(nofuse=True)
                        nc.gpsimd.tensor_tensor(f_lo[:, ic, :], fuse[:, ic % FUSE_RING, :], f_hi[:, ic, :],
                                                ALU.subtract).then_inc(flo_ready, 1)

                    pool.wait_ge(q_sq, since(MS, MS))
                    pool.wait_ge(kq_ready, since(MS, MS))
                    pool.nop(nofuse=True)
                    nc.gpsimd.memset(t_flat, 0.0).then_inc(zero_ready, 1)
                    low_part(0)
                    pool.wait_ge(diag_ready, since(1, 1))
                    for s in range(2):
                        pool.wait_ge(m_ready, since(2, s + 1))
                        if s:
                            pool.wait_ge(t_ready, since(2, 1))
                        pool.nop(nofuse=True)
                        for j in range(SPLIT, CHUNK - 1):
                            rows, cols = CHUNK - 1 - j, j + 1 - SPLIT
                            shape = [P, rows, cols]
                            tmp = outer_p[:, 0:rows * cols].rearrange("p (i c) -> p i c", c=cols)
                            if j > SPLIT:
                                after_last()
                            step(nc.gpsimd.tensor_tensor(tmp, m_prob[:, s, j, j + 1:].unsqueeze(2).to_broadcast(shape),
                                                         t_prob[:, s, j, SPLIT:j + 1].unsqueeze(1).to_broadcast(shape), ALU.mult))
                            after_last()
                            rest = t_prob[:, s, j + 1:, SPLIT:j + 1]
                            ins = nc.gpsimd.tensor_tensor(rest, rest, tmp, ALU.subtract)
                            if j < CHUNK - 2:
                                step(ins)
                            else:
                                ins.then_inc(t_ready, 1)
                            if s == 0 and j in LOW_AT:
                                low_part(LOW_AT[j])
                        if s == 0:
                            for ic in range(1 + len(LOW_AT), LOW_FIRST):
                                low_part(ic)
                    for ic in range(LOW_FIRST, IC):
                        low_part(ic)
                    assert steps[0] == P_STEPS, steps

                    def add_down(j):
                        pool.wait_ge(dn_ready, since(TILES, j + 1))
                        pool.nop(nofuse=True)
                        nc.gpsimd.tensor_tensor(xs[:, par, j, :], xs[:, par, j, :], fuse[:, j % 2, :], ALU.add).then_inc(acc_ready, 1)

                    pool.wait_ge(var_ready, since(1, 2))
                    nc.gpsimd.tensor_tensor(rstd[:, :], var_e[:, :], neg_half[:, 0:TILES], ALU.pow).then_inc(rstd_ready, 1)
                    for j in range(TILES):
                        add_down(j)

            two_spans(0)
            with pool.Fori(1, SPANS // 2) as it:
                two_spans(it)
            count = [0]

            def last_step(ins):
                ins.then_inc(p_step, 1)
                count[0] += 1

            def after_last():
                pool.wait_ge(p_step, P_STEPS * SPANS + count[0])

            o_norm(SPANS // 2, 0, last_step, after_last)
            o_low(SPANS // 2, 0)

        @block.vector
        def _(dve):
            def layer_norm_stats(j, par):
                return nc.vector.bn_stats(stats[:, j, :], xs[:, par, j, :])

            def layer_norm_apply(j, par):
                return nc.vector.tensor_scalar(xn[:, j, :], xs[:, par, j, :], mv[:, j, 0:1], rstd[:, j:j + 1],
                                               ALU.subtract, ALU.mult)

            def low_xt(j, bank):
                nc.vector.tensor_tensor(xt_lo[:, :, j * P:(j + 1) * P], D[bank][:, :].rearrange("p (k n) -> p k n", k=KT_),
                                        xt_hi[:, :, j * P:(j + 1) * P], ALU.subtract).then_inc(xt_lo_ready, 1)

            done = [0]

            def one(ins):
                ins.then_inc(set_v, 1)
                done[0] += 1
                dve.wait_ge(set_v, done[0])

            dve.wait_ge(x_loaded, 32)
            for j in range(TILES):
                one(layer_norm_stats(j, 0))
            for j in range(TILES):
                one(nc.vector.bn_aggr(mv[:, j, :], stats[:, j, :]))
            nc.vector.tensor_scalar(var_e[:, :], mv[:, :, 1], LN_EPS, None, ALU.add).then_inc(var_ready, 1)
            dve.wait_ge(rstd_ready, 1)
            for j in range(TILES):
                layer_norm_apply(j, 0).then_inc(xn_ready, 1)
            for j in range(TILES):
                dve.wait_ge(xt_hi_ready, j + 1)
                low_xt(j, XT_BANKS[j])

            flat = lambda t: t[:, :, :].rearrange("p n d -> p (n d)")
            one(nc.vector.memset(w_hi[:, :, 3 * DM:], 0.0))
            one(nc.vector.memset(w_lo[:, :, 3 * DM:], 0.0))
            dve.wait_ge(small_loaded, 16 * 7)
            dve.wait_ge(w_loaded[4], 16)
            one(nc.vector.tensor_scalar(flat(pt), flat(pt), onw4[:, :], None, ALU.mult))
            for n, src in enumerate((flat(qt), flat(kt), flat(vt), wb_raw[:, :, :].rearrange("p k c -> p (k c)"), flat(pt))):
                dve.wait_ge(w_loaded[n], 16)
                nc.vector.tensor_reduce(amax[:, n:n + 1], src, AX, ALU.max, apply_absolute_value=True).then_inc(amax_ready, 1)
            dve.wait_ge(amax_summed, 1)
            one(nc.vector.tensor_scalar(amax_all[:, :], amax_all[:, :], 2.0 ** -100, None, ALU.max))
            one(nc.vector.tensor_scalar(amax_e[:, :].bitcast(I32), amax_all[:, :].bitcast(I32), 0x7F800000, None, ALU.bitwise_and))
            one(nc.vector.tensor_scalar(w_scale[:, :].bitcast(I32), amax_e[:, :].bitcast(I32), -1.0, float((254 + 13) << 23),
                                        ALU.mult, ALU.add))
            one(nc.vector.tensor_scalar(w_inv[:, :].bitcast(I32), amax_e[:, :].bitcast(I32), float(13 << 23), None, ALU.subtract))
            one(nc.vector.tensor_scalar(q_scale[:, :], w_inv[:, 0:1], float(DH) ** -0.5, None, ALU.mult))
            nc.vector.tensor_scalar(w_inv[:, 3:4], w_inv[:, 3:4], 0.5, None, ALU.mult).then_inc(scales_ready, 1)
            wb_out = lambda w: w[:, :, 3 * DM:].rearrange("p k (h q) -> p k h q", q=32)[:, :, :, 0:MS]
            wb_in = wb_raw[:, :, :].rearrange("p k (m h) -> p k h m", h=QUADS)
            for k in range(KT_):
                one(nc.vector.tensor_scalar(wb_out(w_hi)[:, k], wb_in[:, k], w_scale[:, 3:4], None, ALU.mult))
            for k in range(KT_):
                ins = nc.vector.scalar_tensor_tensor(wb_out(w_lo)[:, k], wb_in[:, k], w_scale[:, 3:4], wb_out(w_hi)[:, k],
                                                     ALU.mult, ALU.subtract)
            ins.then_inc(proj_ready, 1)
            for n, src in enumerate((qt, kt, vt)):
                dve.wait_ge(hi_ready, n + 1)
                nc.vector.scalar_tensor_tensor(w_lo[:, :, n * DM:(n + 1) * DM],
                                               flat(src).rearrange("p (k c) -> p k c", k=KT_), w_scale[:, n:n + 1],
                                               w_hi[:, :, n * DM:(n + 1) * DM], ALU.mult, ALU.subtract).then_inc(proj_ready, 1)
            dve.wait_ge(hi_ready, 4)
            nc.vector.scalar_tensor_tensor(wo_lo[:, :, :], flat(pt).rearrange("p (k c) -> p k c", k=KT_), w_scale[:, 4:5],
                                           wo_hi[:, :, :], ALU.mult, ALU.subtract).then_inc(proj_ready, 1)
            dve.wait_ge(proj_ready, 5)

            def round_piece(n):
                w, c = raw[n % 2], magic[n % 2]
                dve.wait_ge(stage_loaded[n % 2], 16 * (n // 2 + 1))
                one(nc.vector.tensor_scalar(c.bitcast(I32), w.bitcast(I32), 0x7F800000, None, ALU.bitwise_and))
                one(nc.vector.tensor_scalar(c, c, 2.0 ** -6, 1.5 * 2.0 ** 20, ALU.max, ALU.mult))
                one(nc.vector.tensor_tensor(w, w, c, ALU.add))
                return w, c

            for n in range(8):
                w, c = round_piece(n)
                nc.vector.tensor_tensor(wgu[:, n // 2, (n % 2) * INNER:(n % 2 + 1) * INNER], w, c, ALU.subtract).then_inc(wgu_ready, 1)
                dve.wait_ge(wgu_ready, n + 1)
            dve.wait_ge(norms_full, 1)
            one(nc.vector.tensor_copy(bound[:, :], T[0][:, 0:2 * IC]))
            one(nc.vector.tensor_tensor(b_a[:, :], bound[:, 0:IC], bound[:, IC:], ALU.mult))
            for s in (gs, gs, us, us):
                one(nc.vector.tensor_tensor(b_a[:, :], b_a[:, :], s[:, :], ALU.mult))
            nc.vector.tensor_scalar(b_a[:, :], b_a[:, :], float(DM) ** 2, None, ALU.mult).then_inc(bound2_ready, 1)
            dve.wait_ge(bound_ready, 1)
            one(nc.vector.tensor_scalar(b_b[:, :], b_b[:, :], 2.0 ** -60, 2.0 ** 100, ALU.max, ALU.min))
            one(nc.vector.tensor_scalar(b_a[:, :].bitcast(I32), b_b[:, :].bitcast(I32), 0x7F800000, None, ALU.bitwise_and))
            one(nc.vector.tensor_scalar(row_fs[:, :].bitcast(I32), b_a[:, :].bitcast(I32), -1.0, float((254 + 14) << 23), ALU.mult, ALU.add))
            one(nc.vector.tensor_scalar(row_inv[:, :].bitcast(I32), b_a[:, :].bitcast(I32), float(14 << 23), None, ALU.subtract))
            one(nc.vector.tensor_tensor(usf[:, :], us[:, :], row_fs[:, :], ALU.mult))
            for n in range(8, 12):
                w, c = round_piece(n)
                one(nc.vector.tensor_tensor(w, w, c, ALU.subtract))
                for i in range(3):
                    ic = 3 * (n - 8) + i
                    ins = nc.vector.tensor_scalar(wd[:, ic, :], w[:, i * DM:(i + 1) * DM], row_inv[:, ic:ic + 1], None, ALU.mult)
                ins.then_inc(wd_ready, 1)
                dve.wait_ge(wd_ready, n - 7)
            one(nc.vector.memset(state[:, :, :, :], 0.0))
            one(nc.vector.memset(qt[:, :, :], 0.0))
            one(nc.vector.memset(ssq[:, :], 1.0))
            dve.wait_ge(consts, 3 + QUADS)
            nc.vector.memset(xs[:, 1], 0.0).then_inc(ffn_ready, 1)
            dve.wait_ge(ffn_ready, 1)
            per_token = lambda s: s[:, :].unsqueeze(2).to_broadcast([P, MS * BC, DH])

            def o_by_token(it, par):
                dve.wait_ge(o_ready, at_span(it, par, STEPS))
                nc.vector.transpose(o_tok, flat(qt)).then_inc(otok_ready, 1)

            def root_guess(x, y):
                return nc.vector.tensor_scalar(y.bitcast(I32), x.bitcast(I32), -0.5, float(0x5F3759DF), ALU.mult, ALU.add)

            def o_sums(it, par, after, step):
                dve.wait_ge(o_sq, at_span(it, par, 1, 1))
                after(step(nc.vector.tensor_reduce(sso[:, :], pt[:, :, :], AX, ALU.add)))
                after(step(nc.vector.scalar_tensor_tensor(sso[:, :], sso[:, :], 1.0 / DH, ssq[:, :], ALU.mult, ALU.add)))
                root_guess(sso[:, :], ro[:, :]).then_inc(sso_ready, 1)

            def o_scale(it, par, step):
                dve.wait_ge(ro_ready, at_span(it, par, 1, 1))
                o3 = o_tok.rearrange("p (n d) -> p n d", d=DH)
                return step(nc.vector.scalar_tensor_tensor(o3, o3, q_scale[:, :], per_token(ro), ALU.mult, ALU.mult))

            def two_spans(it):
                for par in range(2):
                    def since(per_span, n=0):
                        return at_span(it, par, per_span, n)

                    steps = [0]

                    def step(ins):
                        ins.then_inc(v_step, 1)
                        steps[0] += 1
                        return steps[0]

                    def after(n):
                        dve.wait_ge(v_step, since(V_STEPS, n))

                    def full(job):
                        dve.wait_ge(dense_done, since(DENSE, XT_FIRST + done_dense(job) + 1))
                        return job % 4

                    def group(t, m):
                        return flat(t)[:, m * TOK:(m + 1) * TOK]

                    def to_tokens(job, dst, ready):
                        bank = full(job)
                        nc.vector.transpose(dst, D[bank][:, :]).then_inc(ready, 1)

                    def to_width(m, side):
                        src = (kt, qt)[side]
                        ins = nc.vector.transpose(kq[:, m * BC:(m + 1) * BC, side, :], group(src, m).rearrange("p (n d) -> p n d", d=DH))
                        if side:
                            ins.then_inc(kq_ready, 1)

                    def q_sum(m):
                        dve.wait_ge(q_sq, since(MS, m + 1))
                        step(nc.vector.tensor_reduce(ssq[:, m * BC:(m + 1) * BC], pt[:, m * BC:(m + 1) * BC, :], AX, ALU.add))

                    o_by_token(it, par)
                    to_tokens(JOB_K + 0, group(kt, 0), k_raw)
                    to_tokens(JOB_K + 1, group(kt, 1), k_raw)
                    o_sums(it, par, after, step)
                    to_tokens(JOB_K + 2, group(kt, 2), k_raw)
                    to_tokens(JOB_K + 3, group(kt, 3), k_raw)
                    n = o_scale(it, par, step)
                    dve.wait_ge(k_sq, since(1, 1))
                    k_sum = step(nc.vector.tensor_reduce(ssk[:, :], at[:, :].rearrange("p (n d) -> p n d", d=DH), AX, ALU.add))
                    after(k_sum)
                    k_sum = step(nc.vector.tensor_scalar(ssk[:, :], ssk[:, :], 1e-24, None, ALU.max))
                    after(k_sum)
                    root_guess(ssk[:, :], rk[:, :]).then_inc(ssk_ready, 1)
                    to_tokens(JOB_V + 0, group(vt, 0), v_raw)
                    nc.vector.transpose(kq_flat[:, 0:2048], o_tok).then_inc(ot_ready, 1)
                    for m in range(1, MS):
                        to_tokens(JOB_V + m, group(vt, m), v_raw)
                    dve.wait_ge(rk_ready, since(1, 1))
                    n = step(nc.vector.scalar_tensor_tensor(kt[:, :, :], kt[:, :, :], w_inv[:, 1:2], per_token(rk), ALU.mult, ALU.mult))
                    to_tokens(JOB_B, bt[:, :, :].rearrange("p c q -> p (c q)"), b_raw)
                    after(n)
                    dve.wait_ge(olo_ready, since(1, 1))
                    for m in range(MS):
                        to_width(m, 0)
                    dve.wait_ge(tb_ready, since(1, 1))
                    step(nc.vector.tensor_scalar(beta[:, :], tb[:, :, :].rearrange("p m c -> p (m c)"), 0.5, 0.5, ALU.mult, ALU.add))
                    for m in range(MS):
                        to_tokens(JOB_Q + m, group(qt, m), q_raw)
                        dve.wait_ge(q_raw, since(MS, m + 1))
                        to_width(m, 1)
                        if m:
                            q_sum(m - 1)
                    q_sum(MS - 1)
                    after(steps[0])
                    step(nc.vector.tensor_scalar(ssq[:, :], ssq[:, :], 1e-24, O_EPS, ALU.max, ALU.mult))

                    def fuse_tile(ic):
                        bank = full(gate_up_job(2 * ic + 1))
                        dve.wait_ge(sg_ready, since(IC, ic + 1))
                        dve.wait_ge(flo_ready, since(IC, max(0, ic + 1 - FUSE_RING)))
                        nc.vector.scalar_tensor_tensor(fuse[:, ic % FUSE_RING, :], D[bank][:, :], usf[:, ic:ic + 1], sg[:, ic % 2, :],
                                                       ALU.mult, ALU.mult).then_inc(f_ready, 1)

                    def read_gram(g):
                        dve.wait_ge(tiled_done, since(TILED, g + 1))
                        both = T[g % 4][:, :].rearrange("p (n a t) -> p n a t", n=8, a=2)
                        n0 = 8 * (g % 4)
                        step(nc.vector.tensor_tensor(a_nat[:, g // 4, n0:n0 + 8, :], both[:, :, 0, :],
                                                     beta[:, 8 * g:8 * g + 8].unsqueeze(2).to_broadcast([P, 8, CHUNK]), ALU.mult))
                        nc.vector.tensor_tensor(pt[:, 8 * g:8 * g + 8, :], both[:, :, 1, :],
                                                causal[:, :].unsqueeze(1).to_broadcast([P, 8, CHUNK]), ALU.mult).then_inc(p_ready, 1)

                    def by_problem(s):
                        after(steps[0])
                        nc.vector.transpose(m_prob[:, s], a_nat[:, s].rearrange("p n j -> p j n")).then_inc(m_ready, 1)

                    solved = [0, 0]
                    columns = lambda j: (CHUNK - 1 - j, min(j + 1, SPLIT))

                    def row_products(s, j):
                        shape = [P, *columns(j)]
                        tmp = outer_v[:, 256 * s:256 * s + shape[1] * shape[2]].rearrange("p (i c) -> p i c", c=shape[2])
                        after(solved[s])
                        solved[s] = step(nc.vector.tensor_tensor(tmp, m_prob[:, s, j, j + 1:].unsqueeze(2).to_broadcast(shape),
                                                                 t_prob[:, s, j, 0:shape[2]].unsqueeze(1).to_broadcast(shape), ALU.mult))

                    def off_rows(s, j):
                        rows, cols = columns(j)
                        tmp = outer_v[:, 256 * s:256 * s + rows * cols].rearrange("p (i c) -> p i c", c=cols)
                        rest = t_prob[:, s, j + 1:, 0:cols]
                        after(solved[s])
                        solved[s] = step(nc.vector.tensor_tensor(rest, rest, tmp, ALU.subtract))

                    def solve_steps(j0, j1):
                        for j in range(j0, j1):
                            row_products(0, j)
                            off_rows(0, j)

                    def t_transposed(s):
                        after(solved[s])
                        dve.wait_ge(t_ready, since(2, s + 1))
                        nc.vector.transpose(tt[:, 32 * s:32 * s + 32, :].rearrange("p n t -> p t n"), t_prob[:, s]).then_inc(tt_ready, 1)

                    def read_w(g):
                        dve.wait_ge(tiled_done, since(TILED, DONE_UW + g + 1))
                        nc.vector.transpose(kq[:, 8 * g:8 * g + 8, 0, :],
                                            T[g % 4][:, :].rearrange("p (n a d) -> p n a d", n=8, a=2)[:, :, 0, :]).then_inc(w_ready, 1)
                        if g in (2, 4, 6):
                            fuse_tile(7 + g // 2)

                    def add_out(j):
                        bank = full(JOB_WO + j)
                        y = xs[:, 1 - par, j, :]
                        nc.vector.scalar_tensor_tensor(y, D[bank][:, :], w_inv[:, 4:5], y, ALU.mult, ALU.add).then_inc(wo_added, 1)

                    for g in range(8):
                        read_gram(g)
                        if g in (2, 4, 6):
                            fuse_tile(g // 2 - 1)
                        if g == 3:
                            dve.wait_ge(zero_ready, since(1, 1))
                            for s in range(2):
                                ins = nc.vector.transpose(t_flat[:, 1024 * s:1024 * (s + 1):CHUNK + 1], beta[:, 32 * s:32 * s + 32])
                            ins.then_inc(diag_ready, 1)
                            by_problem(0)
                            dve.wait_ge(diag_ready, since(1, 1))
                            dve.wait_ge(m_ready, since(2, 1))
                        if g > 3:
                            solve_steps(LEAD * (g - 4) // 4, LEAD * (g - 3) // 4)
                    by_problem(1)
                    dve.wait_ge(acc_ready, since(TILES, 0))
                    dve.wait_ge(m_ready, since(2, 2))
                    for j in range(LEAD, CHUNK - 1 + LEAD):
                        sets = [(s, j - s * LEAD) for s in range(2) if j - s * LEAD < CHUNK - 1]
                        for s, i in sets:
                            row_products(s, i)
                        for s, i in sets:
                            off_rows(s, i)
                        if j in OUT_AT:
                            add_out(OUT_AT[j])
                        if j in FUSE_AT:
                            fuse_tile(FUSE_AT[j])
                        if j == CHUNK - 1:
                            t_transposed(0)
                        if j in W_AT:
                            read_w(W_AT[j])
                    t_transposed(1)

                    for g in range(len(W_AT), 8):
                        read_w(g)
                    fuse_tile(IC - 1)

                    def read_down(j):
                        bank = full(JOB_DN + j)
                        if j == 0:
                            dve.wait_ge(flo_ready, since(IC, IC))
                        dve.wait_ge(acc_ready, since(TILES, max(0, j - 1)))
                        nc.vector.tensor_tensor(fuse[:, j % 2, :], D[bank][:, :], ds_row[:, :], ALU.mult).then_inc(dn_ready, 1)

                    for c in range(STEPS):
                        halves = lambda bank: bank[:, :].rearrange("p (b m a t) -> p b m a t", b=BATCH, m=MS, a=2)
                        blocks = lambda tmp: tmp[:, 0:256].rearrange("p (b m t) -> p b m t", b=BATCH, m=MS)
                        dve.wait_ge(tiled_done, since(TILED, DONE_CHAIN + 2 * c + 1))
                        nc.vector.transpose(blocks(outer_v), halves(T[c % 2])[:, :, :, 0, :]).then_inc(ws_read, 1)
                        if c == 0:
                            dve.wait_ge(u_ready, since(8, 8))
                        dve.wait_ge(ws_read, since(STEPS, c + 1))
                        u = u_v[:, :, c]
                        nc.vector.tensor_tensor(u, u, blocks(outer_v), ALU.subtract).then_inc(r_ready, 1)
                        if c == 0:
                            dve.wait_ge(x_loaded, since(32, 64))
                            dve.nop(nofuse=True)
                            step(layer_norm_stats(0, 1 - par))
                            step(layer_norm_stats(1, 1 - par))
                        elif c == 1:
                            step(layer_norm_stats(2, 1 - par))
                            step(layer_norm_stats(3, 1 - par))
                        elif c == 2:
                            after(steps[0])
                            dve.nop(nofuse=True)
                            for j in range(TILES):
                                step(nc.vector.bn_aggr(mv[:, j, :], stats[:, j, :]))
                            after(steps[0])
                            nc.vector.tensor_scalar(var_e[:, :], mv[:, :, 1], LN_EPS, None, ALU.add).then_inc(var_ready, 1)
                        elif c in (3, 4):
                            dve.wait_ge(rstd_ready, since(1, 2))
                            for j in (2 * c - 6, 2 * c - 5):
                                layer_norm_apply(j, 1 - par).then_inc(xn_ready, 1)
                        dve.wait_ge(tiled_done, since(TILED, DONE_CHAIN + 2 * c + 2))
                        n = step(nc.vector.transpose(blocks(outer_p), halves(T[2 + c % 2])[:, :, :, 0, :]))
                        after(n)
                        nc.vector.tensor_tensor(state[:, :, :, :], state[:, :, :, :], blocks(outer_p), ALU.add).then_inc(s_ready, 1)
                        dve.wait_ge(qs_ready, since(STEPS, c + 1))
                        nc.vector.tensor_tensor(ot_v[:, :, c], ot_v[:, :, c], halves(T[2 + c % 2])[:, :, :, 1, :],
                                                ALU.add).then_inc(o_ready, 1)
                        if c in (2, 4, 6):
                            read_down(c // 2 - 1)
                        if c == STEPS - 2:
                            for j in range(TILES):
                                dve.wait_ge(xt_hi_ready, since(TILES, TILES + j + 1))
                                low_xt(j, XT_BANKS[j])
                    read_down(3)
                    assert steps[0] == V_STEPS, steps

            two_spans(0)
            with dve.Fori(1, SPANS // 2) as it:
                two_spans(it)

            o_by_token(SPANS // 2, 0)
            count = [0]

            def last_step(ins):
                ins.then_inc(v_step, 1)
                count[0] += 1
                return count[0]

            def last_after(n):
                dve.wait_ge(v_step, V_STEPS * SPANS + n)

            o_sums(SPANS // 2, 0, last_after, last_step)
            last_after(o_scale(SPANS // 2, 0, last_step))
            nc.vector.transpose(kq_flat[:, 0:2048], o_tok).then_inc(ot_ready, 1)
            dve.wait_ge(acc_ready, TILES * SPANS)
            for j in range(TILES):
                dve.wait_ge(dense_done, XT_FIRST + SPANS * DENSE + j + 1)
                y = xs[:, 1, j, :]
                nc.vector.scalar_tensor_tensor(y, D[j][:, :], w_inv[:, 4:5], y, ALU.mult, ALU.add).then_inc(wo_added, 1)


_INS = ['L0_attn_hidden_states', 'L0_attn_Wq', 'L0_attn_Wk', 'L0_attn_Wv', 'L0_attn_Wb', 'L0_attn_o_norm_weight',
        'L0_attn_Wo', 'L0_ffn_gate_w', 'L0_ffn_up_w', 'L0_ffn_down_w', 'L0_ffn_gate_scale', 'L0_ffn_up_scale',
        'L0_ffn_down_scale']


def kernel(**inputs):
    import numpy as _np
    import concourse.bacc as _bacc
    from concourse import mybir as _mybir
    from concourse.bass_utils import run_bass_kernel_spmd as _run

    nc = _bacc.Bacc("TRN2", target_bir_lowering=False, num_devices=1)
    arrays, args = {}, []
    for name in _INS:
        a = _np.ascontiguousarray(inputs[name])
        arrays[f"in_{name}_dram"] = a
        args.append(nc.dram_tensor(f"in_{name}_dram", a.shape, _mybir.dt.from_np(a.dtype), kind="ExternalInput").ap())
    out = nc.dram_tensor("out_0_dram", (BATCH, LENGTH, DM), _mybir.dt.float32, kind="ExternalOutput").ap()
    delta_block_kernel(nc, *args, out)
    r = _run(nc, [arrays], core_ids=[0])
    return r.results[0]["out_0_dram"]
```

```python
import concourse.bass as bass
from concourse import mybir
from contextlib import ExitStack

BATCH, LENGTH, DM = 2, 4096, 512
HEADS, DH = 16, 32
INNER = 1536
P = 128
SPAN_B = 256
SPANS = LENGTH // SPAN_B
TOK = BATCH * SPAN_B
TILES = TOK // P
CHUNK = 32
STEPS = SPAN_B // CHUNK
BC = BATCH * STEPS
QUADS = P // DH
MS = HEADS // QUADS
KT_ = DM // P
IC = INNER // P
LN_EPS = O_EPS = 1e-05

JOB_K, JOB_V, JOB_B, JOB_Q = 0, MS, 2 * MS, 2 * MS + 1
PROJECTIONS = 3 * MS + 1
GRAMS = MS * BC // 8
JOB_WO = PROJECTIONS + GRAMS
JOB_DN = PROJECTIONS + TILES + 2 * IC
XT_BANKS = [0, 2, 3, 0]
DENSE, XT_FIRST = JOB_DN + 2 * TILES, TILES
DONE_XT = JOB_DN + TILES - 1
DONE_UW, DONE_CHAIN = GRAMS, 2 * GRAMS
TILED = DONE_CHAIN + 2 * STEPS
NEWTONS = 3
SPLIT = 10
V_STEPS = 160
P_STEPS = 2 * (4 * NEWTONS - 1) + 2 * (2 * (CHUNK - 1 - SPLIT) - 1)
LEAD = 14
OUT_AT = {17: 0, 19: 1, 21: 2, 24: 3}
FUSE_AT = {14: 3, 25: 4, 28: 5, 31: 6, 34: 7}
W_AT = {35: 0, 38: 1, 41: 2}
LOW_FIRST = 4
LOW_AT = {18: 1, 30: 2}
FUSE_RING = 4
GU_PIECES, PIECES = 2 * KT_, 2 * KT_ + 4
V_PIECES = 5
SQUARE_ORDER = (5, 6, 7, 0, 1, 2, 3, 4)
UNIT_AT = {1: 4, 2: 5, 3: 6}


def gate_up_job(half):
    return PROJECTIONS + half + (TILES if half >= GRAMS else 0)


def bank_of(job):
    return job % 4 if job < JOB_DN + 3 else JOB_DN % 4


def done_dense(job):
    return job if job < JOB_DN + 3 else DENSE - 1


def delta_block_kernel(nc: bass.Bass, x: bass.AP, wq: bass.AP, wk: bass.AP, wv: bass.AP, wb: bass.AP,
                       onw: bass.AP, wo: bass.AP, gate_w: bass.AP, up_w: bass.AP, down_w: bass.AP,
                       gate_s: bass.AP, up_s: bass.AP, down_s: bass.AP, out: bass.AP):
    F32, F16, BF16, I32 = mybir.dt.float32, mybir.dt.float16, mybir.dt.bfloat16, mybir.dt.int32
    ALU = mybir.AluOpType
    ACT = mybir.ActivationFunctionType
    AX = mybir.AxisListType.X

    x_v = x.rearrange("b (i h p) d -> b i p h d", h=2, p=P)
    out_v = out.rearrange("b (i h p) d -> b i p h d", h=2, p=P)

    ctx = ExitStack()
    with ctx:
        def sb(name, shape, dt=F32):
            return ctx.enter_context(nc.sbuf_tensor(name, shape, dt))

        def sem(name):
            return ctx.enter_context(nc.semaphore(name))

        w_hi = sb("w_hi", [P, KT_, 3 * DM + P], F16)
        w_lo = sb("w_lo", [P, KT_, 3 * DM], F16)
        wo_hi = sb("wo_hi", [P, MS, DM], F16)
        wo_lo = sb("wo_lo", [P, MS, DM], F16)
        wgu = sb("wgu", [P, KT_, 2 * INNER], F16)
        wd = sb("wd", [P, IC, DM], BF16)
        xs = sb("xs", [P, 2, TILES, DM])
        xt_hi = sb("xt_hi", [P, KT_, TOK], F16)
        xt_lo = sb("xt_lo", [P, KT_, TOK], F16)
        f_hi = sb("f_hi", [P, IC, TOK], F16)
        f_lo = sb("f_lo", [P, IC, TOK], F16)
        sg = sb("sg", [P, 2, TOK])
        fuse = sb("fuse", [P, FUSE_RING, TOK])
        kpv = sb("kpv", [P, 3, MS * BC * DH])
        qt = sb("qt", [P, MS * BC, DH])
        kq = sb("kq", [P, MS * BC, 2, CHUNK])
        at = sb("at", [P, 2048])
        mt = sb("mt", [P, 2048])
        outer_v = sb("outer_v", [P, 512])
        outer_p = sb("outer_p", [P, 256])
        state = sb("state", [P, BATCH, MS, DH])
        bt = sb("bt", [P, BC, CHUNK])
        tb = sb("tb", [P, MS, BC])
        beta = sb("beta", [P, MS * BC])
        ssk, ssq, sso = (sb(n, [P, MS * BC]) for n in ("ssk", "ssq", "sso"))
        rk, ro, newton = (sb(n, [P, MS * BC]) for n in ("rk", "ro", "newton"))
        q_scale = sb("q_scale", [P, 1])
        stats = sb("stats", [P, TILES, 6])
        mv = sb("mv", [P, TILES, 2])
        var_e = sb("var_e", [P, TILES])
        rstd = sb("rstd", [P, TILES])
        ident = sb("ident", [P, P])
        causal = sb("causal", [P, CHUNK])
        ones = sb("ones", [P, 1], BF16)
        neg_half = sb("neg_half", [P, MS * BC])
        pos_half = sb("pos_half", [P, IC])
        gs = sb("gs", [P, IC])
        us = sb("us", [P, IC])
        usf = sb("usf", [P, IC])
        row_inv = sb("row_inv", [P, IC])
        row_fs = sb("row_fs", [P, IC])
        bound = sb("bound", [P, 2 * IC])
        b_a = sb("b_a", [P, IC])
        b_b = sb("b_b", [P, IC])
        ds_row = sb("ds_row", [P, DM])
        onw4 = sb("onw4", [P, 1])
        wb_raw = sb("wb_raw", [P, KT_, HEADS])
        amax = sb("amax", [P, 5])
        amax_all = sb("amax_all", [P, 5])
        amax_e = sb("amax_e", [P, 5])
        w_scale = sb("w_scale", [P, 5])
        w_inv = sb("w_inv", [P, 5])

        D = [ctx.enter_context(nc.psum_tensor(f"D{b}", [P, 512], F32)) for b in range(4)]
        T = [ctx.enter_context(nc.psum_tensor(f"T{b}", [P, 512], F32)) for b in range(4)]

        kt, pt, vt = (kpv[:, i, :].rearrange("p (n d) -> p n d", d=DH) for i in range(3))
        t_flat = qt[:, :, :].rearrange("p n d -> p (n d)")
        a_nat = at[:, :].rearrange("p (g n s) -> p g n s", g=2, n=32)
        t_prob = t_flat.rearrange("p (g i c) -> p g i c", g=2, i=CHUNK)
        m_prob = mt[:, :].rearrange("p (g j i) -> p g j i", g=2, j=CHUNK)
        tt = mt[:, :].rearrange("p (n t) -> p n t", t=CHUNK)
        xn = at[:, :].rearrange("p (j d) -> p j d", j=TILES)
        o_hi, o_lo = f_hi[:, IC - MS:, :], f_lo[:, IC - MS:, :]
        kq_flat = kq[:, :, :, :].rearrange("p n a t -> p (n a t)")
        o_t = kq_flat[:, 0:2048].rearrange("p (m n) -> p m n", m=MS)
        o_tok = kq_flat[:, 2048:4096]
        u_v = vt[:, :, :].rearrange("p (m b c) d -> p b c m d", m=MS, b=BATCH)
        ot_v = qt[:, :, :].rearrange("p (m b c) t -> p b c m t", m=MS, b=BATCH)
        f_f32 = f_hi[:, :, :].rearrange("p a b -> p (a b)").bitcast(F32)
        raw = [kq_flat[:, 0:INNER], kq_flat[:, INNER:2 * INNER], f_f32[:, 0:INNER], f_f32[:, INNER:2 * INNER]]
        f_f32 = f_lo[:, :, :].rearrange("p a b -> p (a b)").bitcast(F32)
        magic = [at[:, 0:INNER], mt[:, 0:INNER], f_f32[:, 0:INNER], f_f32[:, INNER:2 * INNER]]
        squares = [fuse[:, 2 * i:2 * i + 2, :].rearrange("p a b -> p (a b)").bitcast(BF16)[:, 0:INNER] for i in range(2)]
        slot = lambda n: n % 2 if n < V_PIECES else 2 + (n - V_PIECES) % 2

        dense_done, tiled_done = sem("dense_done"), sem("tiled_done")
        x_loaded, y_stored = sem("x_loaded"), sem("y_stored")
        w_loaded = [sem(f"w_loaded{n}") for n in range(5)]
        small_loaded = sem("small_loaded")
        stage_loaded = [sem(f"stage_loaded{n}") for n in range(4)]
        v_rounded, p_rounded, wd_ready = sem("v_rounded"), sem("p_rounded"), sem("wd_ready")
        consts = sem("consts")
        amax_ready, amax_summed, scales_ready = sem("amax_ready"), sem("amax_summed"), sem("scales_ready")
        hi_ready, proj_ready = sem("hi_ready"), sem("proj_ready")
        set_p, unit_ready, sq_ready = sem("set_p"), sem("unit_ready"), sem("sq_ready")
        norms_full, bound2_ready, bound_ready, ffn_ready = (
            sem("norms_full"), sem("bound2_ready"), sem("bound_ready"), sem("ffn_ready"))
        set_v = sem("set_v")
        var_ready, rstd_ready, xn_ready = sem("var_ready"), sem("rstd_ready"), sem("xn_ready")
        xt_hi_ready, xt_lo_ready = sem("xt_hi_ready"), sem("xt_lo_ready")
        k_raw, q_raw, v_raw, b_raw = sem("k_raw"), sem("q_raw"), sem("v_raw"), sem("b_raw")
        b_summed = sem("b_summed")
        k_sq, q_sq, tb_ready, v_ready = sem("k_sq"), sem("q_sq"), sem("tb_ready"), sem("v_ready")
        ssk_ready, rk_ready, kq_ready = sem("ssk_ready"), sem("rk_ready"), sem("kq_ready")
        m_ready, zero_ready, diag_ready, t_ready = sem("m_ready"), sem("zero_ready"), sem("diag_ready"), sem("t_ready")
        tt_ready, p_ready = sem("tt_ready"), sem("p_ready")
        u_ready, w_ready, r_ready, s_ready = sem("u_ready"), sem("w_ready"), sem("r_ready"), sem("s_ready")
        ws_read, qs_ready, otok_ready = sem("ws_read"), sem("qs_ready"), sem("otok_ready")
        sg_ready, f_ready, fhi_ready, flo_ready = sem("sg_ready"), sem("f_ready"), sem("fhi_ready"), sem("flo_ready")
        dn_ready, acc_ready, wo_added = sem("dn_ready"), sem("acc_ready"), sem("wo_added")
        o_ready, o_sq, sso_ready, ro_ready = sem("o_ready"), sem("o_sq"), sem("sso_ready"), sem("ro_ready")
        ot_ready, ohi_ready, olo_ready = sem("ot_ready"), sem("ohi_ready"), sem("olo_ready")
        v_step, p_step = sem("v_step"), sem("p_step")

        def at_span(it, par, per_span, n=0):
            return it * (2 * per_span) + (par * per_span + n)

        def round_piece(ops, n, one):
            w, c = raw[slot(n)], magic[slot(n)]
            one(ops.tensor_tensor(w, w, c, ALU.add))
            if n < GU_PIECES:
                dst = wgu[:, n // 2, (n % 2) * INNER:(n % 2 + 1) * INNER]
            else:
                ic = 3 * (n - GU_PIECES)
                dst = wd[:, ic:ic + 3, :].rearrange("p c d -> p (c d)")
            return ops.tensor_tensor(dst, w, c, ALU.subtract)

        block = ctx.enter_context(nc.Block())

        @block.sync
        def _(sp):
            def load_piece(n):
                if n < GU_PIECES:
                    src, dst = (gate_w, up_w)[n % 2][(n // 2) * P:(n // 2 + 1) * P, :], raw[slot(n)]
                else:
                    r = 3 * (n - GU_PIECES) * P
                    src, dst = down_w[r:r + 3 * P, :].rearrange("(c p) d -> p c d", p=P), raw[slot(n)].rearrange("p (c d) -> p c d", c=3)
                sp.dma_start(dst, src).then_inc(stage_loaded[slot(n)], 16)

            for b in range(BATCH):
                sp.dma_start(xs[:, 0, 2 * b:2 * b + 2, :], x_v[b, 0]).then_inc(x_loaded, 16)
            for n, (dst, src) in enumerate(((qt, wq), (kt, wk), (vt, wv))):
                if n in (0, 2):
                    load_piece(V_PIECES + n // 2)
                sp.dma_start(dst[:, :, :].rearrange("p n d -> p (n d)").rearrange("p (k c) -> p k c", k=KT_),
                             src.rearrange("(k p) c -> p k c", p=P)).then_inc(w_loaded[n], 16)
            sp.dma_start(wb_raw[:, :, :], wb.rearrange("(k p) c -> p k c", p=P)).then_inc(w_loaded[3], 16)
            sp.dma_start(pt[:, :, :].rearrange("p n d -> p (n d)").rearrange("p (k c) -> p k c", k=KT_),
                         wo.rearrange("(k p) c -> p k c", p=P)).then_inc(w_loaded[4], 16)
            for h in range(QUADS):
                sp.dma_start(onw4[32 * h:32 * h + 32, :], onw.rearrange("(d o) -> d o", o=1), allow_slow_non_contiguous=True).then_inc(small_loaded, 16)
            sp.dma_start(gs[:, :], gate_s.rearrange("(c p) -> p c", p=P), allow_slow_non_contiguous=True).then_inc(small_loaded, 16)
            sp.dma_start(us[:, :], up_s.rearrange("(c p) -> p c", p=P), allow_slow_non_contiguous=True).then_inc(small_loaded, 16)
            sp.dma_start(ds_row[:, :], down_s.partition_broadcast(P)).then_inc(small_loaded, 16)
            load_piece(0)
            load_piece(1)
            for i in range(2, PIECES - V_PIECES):
                sp.wait_ge(p_rounded, i - 1)
                load_piece(V_PIECES + i)
                if 4 <= i < V_PIECES + 2:
                    sp.wait_ge(v_rounded, i - 3)
                    load_piece(i - 2)

            def load_x(span, par):
                for b in range(BATCH):
                    sp.dma_start(xs[:, par, 2 * b:2 * b + 2, :], x_v[b, span]).then_inc(x_loaded, 16)

            def store_y(span, par):
                for b in range(BATCH):
                    sp.dma_start(out_v[b, span], xs[:, par, 2 * b:2 * b + 2, :]).then_inc(y_stored, 16)

            sp.wait_ge(wo_added, TILES)
            load_x(1, 1)
            with sp.Fori(0, (SPANS - 2) // 2) as it:
                for par in range(2):
                    sp.wait_ge(wo_added, at_span(it, par, TILES, 2 * TILES))
                    sp.nop(nofuse=True)
                    store_y(it * 2 + par, par)
                    sp.wait_ge(y_stored, at_span(it, par, 32, 32))
                    sp.nop(nofuse=True)
                    load_x(it * 2 + (par + 2), par)
            sp.wait_ge(wo_added, TILES * SPANS)
            store_y(SPANS - 2, 0)
            sp.wait_ge(y_stored, 32 * (SPANS - 1))
            load_x(0, 0)
            sp.wait_ge(wo_added, TILES * (SPANS + 1))
            store_y(SPANS - 1, 1)
            sp.wait_ge(y_stored, 32 * SPANS)
            sp.wait_ge(x_loaded, 32 * (SPANS + 1))

        @block.tensor
        def _(pe):
            def quads(out, lhs, rhs, start=True, stop=True):
                for h in range(QUADS):
                    s = slice(32 * h, 32 * h + 32)
                    last = nc.tensor.matmul(out[s], lhs[s], rhs[s], start=start, stop=stop)
                return last

            def transpose_xn(j, bank):
                for k in range(KT_):
                    last = nc.tensor.transpose(D[bank][:, k * P:(k + 1) * P], xn[:, j, k * P:(k + 1) * P], ident[:, :])
                last.then_inc(dense_done, 1)

            def project_out(j, bank, last=False):
                n = 0
                for m in range(MS):
                    if last:
                        pe.wait_ge(olo_ready, SPANS + m + 1)
                    for o_part, w in ((o_hi, wo_hi), (o_lo, wo_hi), (o_hi, wo_lo)):
                        ins = nc.tensor.matmul(D[bank][:, :], o_part[:, m, j * P:(j + 1) * P], w[:, m, :],
                                                start=n == 0, stop=n == 3 * MS - 1)
                        n += 1
                ins.then_inc(dense_done, 1)

            pe.wait_ge(consts, 2)
            for j in range(TILES):
                b = XT_BANKS[j]
                pe.wait_ge(xn_ready, j + 1)
                if j == 3:
                    pe.wait_ge(xt_lo_ready, 1)
                transpose_xn(j, b)
            for i, n in enumerate(SQUARE_ORDER):
                pe.wait_ge(sq_ready, i + 1)
                for c in range(IC):
                    last = nc.tensor.matmul(T[0][:, 12 * n + c:12 * n + c + 1], squares[i % 2][:, c * P:(c + 1) * P], ones[:, :],
                                            start=True, stop=True)
                last.then_inc(norms_full, 1)
            pe.wait_ge(proj_ready, 5)
            pe.wait_ge(ffn_ready, 1)

            def two_spans(it):
                for par in range(2):
                    def since(per_span, n=0):
                        return at_span(it, par, per_span, n)

                    def take(job):
                        before = job - 4
                        if before < 0:
                            pe.wait_ge(*((dn_ready, since(TILES)) if job == 1 else (xt_lo_ready, since(TILES, TILES))))
                        elif job == JOB_DN + 3:
                            pe.wait_ge(dn_ready, since(TILES, 1))
                        elif before < JOB_V:
                            pe.wait_ge(k_raw, since(MS, before + 1))
                        elif before < JOB_B:
                            pe.wait_ge(v_raw, since(MS, before - JOB_V + 1))
                        elif before < JOB_Q:
                            pe.wait_ge(b_raw, since(1, 1))
                        elif before < PROJECTIONS:
                            pe.wait_ge(q_raw, since(MS, before - JOB_Q + 1))
                        elif JOB_WO <= before < JOB_WO + TILES:
                            pe.wait_ge(wo_added, since(TILES, before - JOB_WO + 1))
                        else:
                            half = before - (PROJECTIONS if before < JOB_WO else PROJECTIONS + TILES)
                            pe.wait_ge(f_ready if half % 2 else sg_ready, since(IC, half // 2 + 1))
                        return bank_of(job)

                    pe.wait_ge(xt_lo_ready, since(TILES, TILES))
                    for job in range(PROJECTIONS):
                        g = (4, 5, 6, 7, 8, 9, 10, 11, 12, 0, 1, 2, 3)[job]
                        bank = take(job)
                        cols = slice(g * P, (g + 1) * P)
                        parts = ((w_hi, xt_hi), (w_hi, xt_lo), (w_lo, xt_hi))[:2 if job == JOB_B else 3]
                        n = 0
                        for k in range(KT_):
                            for w, xp in parts:
                                last = nc.tensor.matmul(D[bank][:, :], w[:, k, cols], xp[:, k, :],
                                                        start=n == 0, stop=n == len(parts) * KT_ - 1)
                                n += 1
                        last.then_inc(dense_done, 1)

                    def gate_up(half):
                        bank = take(gate_up_job(half))
                        ic, side = divmod(half, 2)
                        c = side * INNER + ic * P
                        for k in range(KT_):
                            nc.tensor.matmul(D[bank][:, :], wgu[:, k, c:c + P], xt_hi[:, k, :], start=k == 0, stop=False)
                            last = nc.tensor.matmul(D[bank][:, :], wgu[:, k, c:c + P], xt_lo[:, k, :],
                                                    start=False, stop=k == KT_ - 1)
                        last.then_inc(dense_done, 1)

                    def gram(g):
                        pe.wait_ge(kq_ready, since(MS, g // 2 + 1))
                        if g < 4:
                            pe.wait_ge(qs_ready if g < 2 else o_ready, since(STEPS))
                        else:
                            pe.wait_ge(p_ready, since(8, g - 3))
                        pe.nop(nofuse=True)
                        for n in range(8):
                            both = kq_flat.rearrange("p (n t) -> p n t", t=2 * CHUNK)[:, 8 * g + n, :]
                            last = quads(T[g % 4][:, 64 * n:64 * n + 64], both[:, 0:CHUNK], both)
                        last.then_inc(tiled_done, 1)

                    pe.wait_ge(p_rounded, GU_PIECES - V_PIECES)
                    for g in range(8):
                        gram(g)
                        gate_up(g)
                    pe.wait_ge(olo_ready, since(1, 1))
                    for j in range(TILES):
                        project_out(j, take(JOB_WO + j))
                    for half in range(8, 16):
                        gate_up(half)

                    pe.wait_ge(v_ready, since(1, 1))
                    for g in range(8):
                        pe.wait_ge(tt_ready, since(2, g // 4 + 1))
                        pe.wait_ge(*((u_ready, since(8, g - 3)) if g >= 4 else (p_ready, since(8, g + 5))))
                        pe.nop(nofuse=True)
                        for n in range(8):
                            pc = 8 * g + n
                            last = quads(T[g % 4][:, 64 * n:64 * n + 64], tt[:, pc, :], kpv[:, 0:3:2, pc * DH:(pc + 1) * DH])
                        last.then_inc(tiled_done, 1)
                        gate_up(16 + g)

                    def down(j, part):
                        bank = bank_of(JOB_DN + j)
                        if j == 0:
                            pe.wait_ge(flo_ready, since(IC, 3 * part + 3))
                            pe.wait_ge(wd_ready, 1)
                        for ic in range(3 * part, 3 * part + 3):
                            nc.tensor.matmul(D[bank][:, :], f_hi[:, ic, j * P:(j + 1) * P], wd[:, ic, :], start=ic == 0, stop=False)
                            last = nc.tensor.matmul(D[bank][:, :], f_lo[:, ic, j * P:(j + 1) * P], wd[:, ic, :],
                                                    start=False, stop=ic == IC - 1)
                        if part == 3:
                            last.then_inc(dense_done, 1)

                    def transpose_next(j):
                        pe.wait_ge(xn_ready, since(TILES, TILES + j + 1))
                        pe.wait_ge(*((f_ready, since(IC, IC)), (dn_ready, since(TILES, 2)), (dn_ready, since(TILES, 3)),
                                     (xt_lo_ready, since(TILES, TILES + 1)))[j])
                        transpose_xn(j, XT_BANKS[j])

                    for c in range(STEPS):
                        if c == 0:
                            pe.wait_ge(w_ready, since(8, 8))
                        pe.wait_ge(s_ready, since(STEPS, c))
                        pe.wait_ge(*((qs_ready, since(STEPS, c - 1)) if c >= 2 else (u_ready, since(8, 8))))
                        pe.nop(nofuse=True)
                        for b in range(BATCH):
                            for m in range(MS):
                                n, pc = b * MS + m, m * BC + b * STEPS + c
                                last = quads(T[c % 2][:, 64 * n:64 * n + 64], state[:, b, m, :],
                                             kq_flat[:, 64 * pc:64 * pc + 64])
                        last.then_inc(tiled_done, 1)
                        if c % 2 == 0:
                            take(JOB_DN + c // 2)
                        down(c // 2, 2 * (c % 2))
                        if c == STEPS - 1:
                            transpose_next(TILES - 1)
                        pe.wait_ge(r_ready, since(STEPS, c + 1))
                        if c >= 2:
                            pe.wait_ge(o_ready, since(STEPS, c - 1))
                        pe.nop(nofuse=True)
                        for b in range(BATCH):
                            for m in range(MS):
                                n, pc = b * MS + m, m * BC + b * STEPS + c
                                last = quads(T[2 + c % 2][:, 64 * n:64 * n + 64], vt[:, pc, :],
                                             kpv[:, 0:2, pc * DH:(pc + 1) * DH])
                        last.then_inc(tiled_done, 1)
                        down(c // 2, 2 * (c % 2) + 1)
                        if c == STEPS - 2:
                            for j in range(TILES - 1):
                                transpose_next(j)

            two_spans(0)
            with pe.Fori(1, SPANS // 2) as it:
                two_spans(it)

            pe.wait_ge(dn_ready, TILES * SPANS)
            pe.wait_ge(xt_lo_ready, TILES * (SPANS + 1))
            for j in range(TILES):
                project_out(j, j, last=True)

        @block.scalar
        def _(act):
            def evacuate_xt(j, bank):
                nc.scalar.activation(xt_hi[:, :, j * P:(j + 1) * P], D[bank][:, :].rearrange("p (k n) -> p k n", k=KT_),
                                     ACT.Copy).then_inc(xt_hi_ready, 1)

            for j in range(TILES):
                act.wait_ge(dense_done, j + 1)
                evacuate_xt(j, XT_BANKS[j])
            act.wait_ge(scales_ready, 1)
            for n, src in enumerate((qt, kt, vt)):
                nc.scalar.activation(w_hi[:, :, n * DM:(n + 1) * DM],
                                     src[:, :, :].rearrange("p n d -> p (n d)").rearrange("p (k c) -> p k c", k=KT_),
                                     ACT.Identity, scale=w_scale[:, n:n + 1]).then_inc(hi_ready, 1)
            nc.scalar.activation(wo_hi[:, :, :], pt[:, :, :].rearrange("p n d -> p (n d)").rearrange("p (k c) -> p k c", k=KT_),
                                 ACT.Identity, scale=w_scale[:, 4:5]).then_inc(hi_ready, 1)
            for i, n in enumerate(SQUARE_ORDER):
                if n < V_PIECES:
                    act.wait_ge(v_rounded, n + 1)
                else:
                    act.wait_ge(p_rounded, n - V_PIECES + 1)
                if i >= 2:
                    act.wait_ge(norms_full, i - 1)
                nc.scalar.activation(squares[i % 2], wgu[:, n // 2, (n % 2) * INNER:(n % 2 + 1) * INNER],
                                     ACT.Square).then_inc(sq_ready, 1)
            act.wait_ge(ffn_ready, 1)
            flat = lambda t: t[:, :, :].rearrange("p n d -> p (n d)")

            def o_squares(it, par):
                act.wait_ge(otok_ready, at_span(it, par, 1, 1))
                nc.scalar.activation(flat(pt), o_tok, ACT.Square, scale=q_scale[:, :]).then_inc(o_sq, 1)

            def o_high(it, par):
                act.wait_ge(ot_ready, at_span(it, par, 1, 1))
                nc.scalar.activation(o_hi, o_t, ACT.Copy).then_inc(ohi_ready, 1)

            def two_spans(it, first=False):
                for par in range(2):
                    def since(per_span, n=0):
                        return at_span(it, par, per_span, n)

                    def full(job):
                        act.wait_ge(dense_done, since(DENSE, XT_FIRST + done_dense(job) + 1))
                        return bank_of(job)

                    o_squares(it, par)
                    act.wait_ge(k_raw, since(MS, MS))
                    nc.scalar.activation(at[:, :], flat(kt), ACT.Square, scale=w_inv[:, 1:2]).then_inc(k_sq, 1)
                    o_high(it, par)
                    act.wait_ge(v_raw, since(MS, MS))
                    nc.scalar.activation(flat(vt), flat(vt), ACT.Silu, scale=w_inv[:, 2:3]).then_inc(v_ready, 1)
                    act.wait_ge(b_summed, since(1, 1))
                    nc.scalar.activation(tb[:, :, :], tb[:, :, :], ACT.Tanh, scale=w_inv[:, 3:4]).then_inc(tb_ready, 1)
                    for m in range(MS):
                        act.wait_ge(q_raw, since(MS, m + 1))
                        nc.scalar.activation(flat(pt)[:, m * TOK:(m + 1) * TOK], flat(qt)[:, m * TOK:(m + 1) * TOK],
                                             ACT.Square, scale=w_inv[:, 0:1]).then_inc(q_sq, 1)

                    def high_part(ic):
                        act.wait_ge(f_ready, since(IC, ic + 1))
                        nc.scalar.activation(f_hi[:, ic, :], fuse[:, ic % FUSE_RING, :], ACT.Copy).then_inc(fhi_ready, 1)

                    def silu_gate(ic):
                        bank = full(gate_up_job(2 * ic))
                        nc.scalar.activation(sg[:, ic % 2, :], D[bank][:, :], ACT.Silu,
                                             scale=gs[:, ic:ic + 1]).then_inc(sg_ready, 1)
                        if ic % 8:
                            high_part(ic - 1)

                    def copy_u(g):
                        act.wait_ge(w_ready, since(8, g + 1))
                        nc.scalar.activation(vt[:, 8 * g:8 * g + 8, :],
                                             T[g % 4][:, :].rearrange("p (n a d) -> p n a d", n=8, a=2)[:, :, 1, :],
                                             ACT.Copy).then_inc(u_ready, 1)

                    for ic in range(8):
                        silu_gate(ic)
                    high_part(7)
                    if first and par == 0:
                        act.wait_ge(p_rounded, PIECES - V_PIECES)
                        for ic in range(IC):
                            ins = nc.scalar.activation(wd[:, ic, :], wd[:, ic, :], ACT.Identity, scale=row_inv[:, ic:ic + 1])
                        ins.then_inc(wd_ready, 1)
                    for g in range(8):
                        copy_u(g)
                        if g % 2 == 0:
                            silu_gate(8 + g // 2)
                    high_part(IC - 1)
                    for c in range(STEPS):
                        act.wait_ge(ws_read, since(STEPS, c + 1))
                        nc.scalar.activation(ot_v[:, :, c], T[c % 2][:, :].rearrange("p (b m a t) -> p b m a t", b=BATCH, m=MS, a=2)[:, :, :, 1, :],
                                             ACT.Copy).then_inc(qs_ready, 1)
                        for j in {STEPS - 2: range(TILES - 1), STEPS - 1: (TILES - 1,)}.get(c, ()):
                            act.wait_ge(dense_done, since(DENSE, XT_FIRST + DONE_XT + j + 1))
                            evacuate_xt(j, XT_BANKS[j])

            two_spans(0, first=True)
            with act.Fori(1, SPANS // 2) as it:
                two_spans(it)
            for m in range(MS):
                group = slice(m * TOK, (m + 1) * TOK)
                act.wait_ge(otok_ready, SPANS + m + 1)
                nc.scalar.activation(flat(pt)[:, group], o_tok[:, group], ACT.Square, scale=q_scale[:, :]).then_inc(o_sq, 1)
            for m in range(MS):
                act.wait_ge(ot_ready, SPANS + m + 1)
                nc.scalar.activation(o_hi[:, m, :], o_t[:, m, :], ACT.Copy).then_inc(ohi_ready, 1)

        @block.gpsimd
        def _(pool):
            nc.gpsimd.memset(ident[:, :], 0.0).then_inc(consts, 1)
            pool.wait_ge(consts, 1)
            nc.gpsimd.affine_select(out=ident[:, :], in_=ident[:, :], compare_op=ALU.not_equal, fill=1.0, base=0,
                                    pattern=[[-1, P]], channel_multiplier=1).then_inc(consts, 1)
            nc.gpsimd.memset(neg_half[:, :], -0.5)
            nc.gpsimd.memset(pos_half[:, :], 0.5)
            nc.gpsimd.memset(ones[:, :], 1.0)
            nc.gpsimd.memset(causal[:, :], 1.0).then_inc(consts, 1)
            pool.wait_ge(consts, 3)
            for h in range(QUADS):
                c = causal[32 * h:32 * h + 32, :]
                nc.gpsimd.affine_select(out=c, in_=c, compare_op=ALU.is_ge, fill=0.0, base=0,
                                        pattern=[[1, CHUNK]], channel_multiplier=-1).then_inc(consts, 1)
                pool.wait_ge(consts, 4 + h)
            done = [0]

            def one(ins):
                ins.then_inc(set_p, 1)
                done[0] += 1
                pool.wait_ge(set_p, done[0])

            nc.gpsimd.memset(xs[:, 1], 0.0).then_inc(consts, 1)
            pool.wait_ge(var_ready, 1)
            nc.gpsimd.tensor_tensor(rstd[:, :], var_e[:, :], neg_half[:, 0:TILES], ALU.pow).then_inc(rstd_ready, 1)
            for n in range(V_PIECES, V_PIECES + 2):
                pool.wait_ge(unit_ready, n - V_PIECES + 1)
                round_piece(nc.gpsimd, n, one).then_inc(p_rounded, 1)
            pool.wait_ge(amax_ready, 5)
            nc.gpsimd.partition_all_reduce(amax_all[:, :], amax[:, :], P, bass.bass_isa.ReduceOp.absmax).then_inc(amax_summed, 1)
            for n in range(V_PIECES + 2, PIECES):
                pool.wait_ge(unit_ready, n - V_PIECES + 1)
                round_piece(nc.gpsimd, n, one).then_inc(p_rounded, 1)
            pool.wait_ge(bound2_ready, 1)
            nc.gpsimd.tensor_tensor(b_b[:, :], b_a[:, :], pos_half[:, :], ALU.pow).then_inc(bound_ready, 1)

            def inverse_root(x, y, step, after_last):
                for n in range(NEWTONS):
                    if n:
                        after_last()
                    step(nc.gpsimd.tensor_tensor(newton[:, :], y, y, ALU.mult))
                    after_last()
                    step(nc.gpsimd.tensor_tensor(newton[:, :], newton[:, :], x, ALU.mult))
                    after_last()
                    step(nc.gpsimd.tensor_scalar(newton[:, :], newton[:, :], -0.5, 1.5, ALU.mult, ALU.add))
                    after_last()
                    last = nc.gpsimd.tensor_tensor(y, y, newton[:, :], ALU.mult)
                    if n < NEWTONS - 1:
                        step(last)
                return last

            def o_norm(it, par, step, after_last):
                pool.wait_ge(sso_ready, at_span(it, par, 1, 1))
                inverse_root(sso[:, :], ro[:, :], step, after_last).then_inc(ro_ready, 1)

            def o_low(it, par):
                pool.wait_ge(ohi_ready, at_span(it, par, 1, 1))
                nc.gpsimd.tensor_tensor(o_lo, o_t, o_hi, ALU.subtract).then_inc(olo_ready, 1)

            def two_spans(it):
                for par in range(2):
                    def since(per_span, n=0):
                        return at_span(it, par, per_span, n)

                    steps = [0]

                    def step(ins):
                        ins.then_inc(p_step, 1)
                        steps[0] += 1

                    def after_last():
                        pool.wait_ge(p_step, since(P_STEPS, steps[0]))
                        pool.nop(nofuse=True)

                    o_norm(it, par, step, after_last)
                    pool.wait_ge(ssk_ready, since(1, 1))
                    inverse_root(ssk[:, :], rk[:, :], step, after_last).then_inc(rk_ready, 1)
                    o_low(it, par)

                    def low_part(ic):
                        pool.wait_ge(fhi_ready, since(IC, ic + 1))
                        pool.nop(nofuse=True)
                        nc.gpsimd.tensor_tensor(f_lo[:, ic, :], fuse[:, ic % FUSE_RING, :], f_hi[:, ic, :],
                                                ALU.subtract).then_inc(flo_ready, 1)

                    pool.wait_ge(q_sq, since(MS, MS))
                    pool.wait_ge(kq_ready, since(MS, MS))
                    pool.nop(nofuse=True)
                    nc.gpsimd.memset(t_flat, 0.0).then_inc(zero_ready, 1)
                    low_part(0)
                    pool.wait_ge(diag_ready, since(1, 1))
                    for s in range(2):
                        pool.wait_ge(m_ready, since(2, s + 1))
                        if s:
                            pool.wait_ge(t_ready, since(2, 1))
                        pool.nop(nofuse=True)
                        for j in range(SPLIT, CHUNK - 1):
                            rows, cols = CHUNK - 1 - j, j + 1 - SPLIT
                            shape = [P, rows, cols]
                            tmp = outer_p[:, 0:rows * cols].rearrange("p (i c) -> p i c", c=cols)
                            if j > SPLIT:
                                after_last()
                            step(nc.gpsimd.tensor_tensor(tmp, m_prob[:, s, j, j + 1:].unsqueeze(2).to_broadcast(shape),
                                                         t_prob[:, s, j, SPLIT:j + 1].unsqueeze(1).to_broadcast(shape), ALU.mult))
                            after_last()
                            rest = t_prob[:, s, j + 1:, SPLIT:j + 1]
                            ins = nc.gpsimd.tensor_tensor(rest, rest, tmp, ALU.subtract)
                            if j < CHUNK - 2:
                                step(ins)
                            else:
                                ins.then_inc(t_ready, 1)
                            if s == 0 and j in LOW_AT:
                                low_part(LOW_AT[j])
                        if s == 0:
                            for ic in range(1 + len(LOW_AT), LOW_FIRST):
                                low_part(ic)
                    for ic in range(LOW_FIRST, IC):
                        low_part(ic)
                    assert steps[0] == P_STEPS, steps

                    def add_down(j):
                        pool.wait_ge(dn_ready, since(TILES, j + 1))
                        pool.nop(nofuse=True)
                        nc.gpsimd.tensor_tensor(xs[:, par, j, :], xs[:, par, j, :], fuse[:, j % 2, :], ALU.add).then_inc(acc_ready, 1)

                    pool.wait_ge(var_ready, since(1, 2))
                    nc.gpsimd.tensor_tensor(rstd[:, :], var_e[:, :], neg_half[:, 0:TILES], ALU.pow).then_inc(rstd_ready, 1)
                    for j in range(TILES):
                        add_down(j)

            two_spans(0)
            with pool.Fori(1, SPANS // 2) as it:
                two_spans(it)

        @block.vector
        def _(dve):
            def layer_norm_stats(j, par):
                return nc.vector.bn_stats(stats[:, j, :], xs[:, par, j, :])

            def layer_norm_apply(j, par):
                return nc.vector.tensor_scalar(xn[:, j, :], xs[:, par, j, :], mv[:, j, 0:1], rstd[:, j:j + 1],
                                               ALU.subtract, ALU.mult)

            def low_xt(j, bank):
                nc.vector.tensor_tensor(xt_lo[:, :, j * P:(j + 1) * P], D[bank][:, :].rearrange("p (k n) -> p k n", k=KT_),
                                        xt_hi[:, :, j * P:(j + 1) * P], ALU.subtract).then_inc(xt_lo_ready, 1)

            done = [0]

            def one(ins):
                ins.then_inc(set_v, 1)
                done[0] += 1
                dve.wait_ge(set_v, done[0])

            dve.wait_ge(x_loaded, 32)
            for j in range(TILES):
                one(layer_norm_stats(j, 0))
            for j in range(TILES):
                one(nc.vector.bn_aggr(mv[:, j, :], stats[:, j, :]))
            nc.vector.tensor_scalar(var_e[:, :], mv[:, :, 1], LN_EPS, None, ALU.add).then_inc(var_ready, 1)
            dve.wait_ge(rstd_ready, 1)
            for j in range(TILES):
                layer_norm_apply(j, 0).then_inc(xn_ready, 1)
            for j in range(TILES):
                dve.wait_ge(xt_hi_ready, j + 1)
                low_xt(j, XT_BANKS[j])

            def rounding_unit(n):
                w, c = raw[slot(n)], magic[slot(n)]
                i = n if n < V_PIECES else n - V_PIECES
                dve.wait_ge(stage_loaded[slot(n)], 16 * (i // 2 + 1))
                one(nc.vector.tensor_scalar(c.bitcast(I32), w.bitcast(I32), 0x7F800000, None, ALU.bitwise_and))
                return nc.vector.tensor_scalar(c, c, 2.0 ** -6, 1.5 * 2.0 ** 20, ALU.max, ALU.mult)

            def p_unit(i):
                if i >= 2:
                    dve.wait_ge(p_rounded, i - 1)
                rounding_unit(V_PIECES + i).then_inc(unit_ready, 1)

            flat = lambda t: t[:, :, :].rearrange("p n d -> p (n d)")
            one(nc.vector.memset(w_hi[:, :, 3 * DM:], 0.0))
            for n, src in enumerate((flat(qt), flat(kt), flat(vt), wb_raw[:, :, :].rearrange("p k c -> p (k c)"), flat(pt))):
                if n in (0, 2, 4):
                    p_unit(n // 2)
                dve.wait_ge(w_loaded[n], 16)
                if n == 4:
                    dve.wait_ge(small_loaded, 16 * 7)
                    one(nc.vector.tensor_scalar(flat(pt), flat(pt), onw4[:, :], None, ALU.mult))
                nc.vector.tensor_reduce(amax[:, n:n + 1], src, AX, ALU.max, apply_absolute_value=True).then_inc(amax_ready, 1)
            dve.wait_ge(amax_summed, 1)
            one(nc.vector.tensor_scalar(amax_all[:, :], amax_all[:, :], 2.0 ** -100, None, ALU.max))
            one(nc.vector.tensor_scalar(amax_e[:, :].bitcast(I32), amax_all[:, :].bitcast(I32), 0x7F800000, None, ALU.bitwise_and))
            one(nc.vector.tensor_scalar(w_scale[:, :].bitcast(I32), amax_e[:, :].bitcast(I32), -1.0, float((254 + 13) << 23),
                                        ALU.mult, ALU.add))
            one(nc.vector.tensor_scalar(w_inv[:, :].bitcast(I32), amax_e[:, :].bitcast(I32), float(13 << 23), None, ALU.subtract))
            one(nc.vector.tensor_scalar(q_scale[:, :], w_inv[:, 0:1], float(DH) ** -0.5, None, ALU.mult))
            nc.vector.tensor_scalar(w_inv[:, 3:4], w_inv[:, 3:4], 0.5, None, ALU.mult).then_inc(scales_ready, 1)
            wb_out = w_hi[:, :, 3 * DM:].rearrange("p k (h q) -> p k h q", q=32)
            wb_in = wb_raw[:, :, :].rearrange("p k (m h) -> p k h m", h=QUADS)
            for k in range(KT_):
                one(nc.vector.tensor_scalar(wb_out[:, k, :, 0:MS], wb_in[:, k], w_scale[:, 3:4], None, ALU.mult))
            for k in range(KT_):
                ins = nc.vector.scalar_tensor_tensor(wb_out[:, k, :, MS:2 * MS], wb_in[:, k], w_scale[:, 3:4],
                                                     wb_out[:, k, :, 0:MS], ALU.mult, ALU.subtract)
            ins.then_inc(proj_ready, 1)
            for n, src in enumerate((qt, kt, vt)):
                dve.wait_ge(hi_ready, n + 1)
                nc.vector.scalar_tensor_tensor(w_lo[:, :, n * DM:(n + 1) * DM],
                                               flat(src).rearrange("p (k c) -> p k c", k=KT_), w_scale[:, n:n + 1],
                                               w_hi[:, :, n * DM:(n + 1) * DM], ALU.mult, ALU.subtract).then_inc(proj_ready, 1)
                if n == 2:
                    p_unit(3)
            dve.wait_ge(hi_ready, 4)
            nc.vector.scalar_tensor_tensor(wo_lo[:, :, :], flat(pt).rearrange("p (k c) -> p k c", k=KT_), w_scale[:, 4:5],
                                           wo_hi[:, :, :], ALU.mult, ALU.subtract).then_inc(proj_ready, 1)
            dve.wait_ge(proj_ready, 5)

            for n in range(V_PIECES):
                one(rounding_unit(n))
                round_piece(nc.vector, n, one).then_inc(v_rounded, 1)
                dve.wait_ge(v_rounded, n + 1)
                if n in UNIT_AT:
                    p_unit(UNIT_AT[n])
            one(nc.vector.memset(state[:, :, :, :], 0.0))
            dve.wait_ge(consts, 4 + QUADS)
            nc.vector.memset(ssq[:, :], 1.0).then_inc(ffn_ready, 1)
            dve.wait_ge(ffn_ready, 1)
            per_token = lambda s: s[:, :].unsqueeze(2).to_broadcast([P, MS * BC, DH])

            def o_by_token(it, par):
                dve.wait_ge(o_ready, at_span(it, par, STEPS))
                nc.vector.transpose(o_tok, flat(qt)).then_inc(otok_ready, 1)

            def gate_up_bound():
                dve.wait_ge(norms_full, GU_PIECES)
                one(nc.vector.tensor_reduce(bound[:, :], T[0][:, 0:2 * IC * KT_].rearrange("p (k c) -> p c k", k=KT_), AX, ALU.add))
                one(nc.vector.tensor_tensor(b_a[:, :], bound[:, 0:IC], bound[:, IC:], ALU.mult))
                for s in (gs, gs, us, us):
                    one(nc.vector.tensor_tensor(b_a[:, :], b_a[:, :], s[:, :], ALU.mult))
                nc.vector.tensor_scalar(b_a[:, :], b_a[:, :], float(DM) ** 2, None, ALU.mult).then_inc(bound2_ready, 1)

            def gate_up_scale():
                dve.wait_ge(bound_ready, 1)
                one(nc.vector.tensor_scalar(b_b[:, :], b_b[:, :], 2.0 ** -60, 2.0 ** 100, ALU.max, ALU.min))
                one(nc.vector.tensor_scalar(b_a[:, :].bitcast(I32), b_b[:, :].bitcast(I32), 0x7F800000, None, ALU.bitwise_and))
                one(nc.vector.tensor_scalar(row_fs[:, :].bitcast(I32), b_a[:, :].bitcast(I32), -1.0, float((254 + 14) << 23), ALU.mult, ALU.add))
                one(nc.vector.tensor_scalar(row_inv[:, :].bitcast(I32), b_a[:, :].bitcast(I32), float(14 << 23), None, ALU.subtract))
                one(nc.vector.tensor_tensor(usf[:, :], us[:, :], row_fs[:, :], ALU.mult))

            def root_guess(x, y):
                return nc.vector.tensor_scalar(y.bitcast(I32), x.bitcast(I32), -0.5, float(0x5F3759DF), ALU.mult, ALU.add)

            def o_sums(it, par, after, step):
                dve.wait_ge(o_sq, at_span(it, par, 1, 1))
                after(step(nc.vector.tensor_reduce(sso[:, :], pt[:, :, :], AX, ALU.add)))
                after(step(nc.vector.scalar_tensor_tensor(sso[:, :], sso[:, :], 1.0 / DH, ssq[:, :], ALU.mult, ALU.add)))
                root_guess(sso[:, :], ro[:, :]).then_inc(sso_ready, 1)

            def o_scale(it, par, step):
                dve.wait_ge(ro_ready, at_span(it, par, 1, 1))
                o3 = o_tok.rearrange("p (n d) -> p n d", d=DH)
                return step(nc.vector.scalar_tensor_tensor(o3, o3, q_scale[:, :], per_token(ro), ALU.mult, ALU.mult))

            def two_spans(it, first=False):
                for par in range(2):
                    def since(per_span, n=0):
                        return at_span(it, par, per_span, n)

                    steps = [0]

                    def step(ins):
                        ins.then_inc(v_step, 1)
                        steps[0] += 1
                        return steps[0]

                    def after(n):
                        dve.wait_ge(v_step, since(V_STEPS, n))

                    def full(job):
                        dve.wait_ge(dense_done, since(DENSE, XT_FIRST + done_dense(job) + 1))
                        return bank_of(job)

                    def group(t, m):
                        return flat(t)[:, m * TOK:(m + 1) * TOK]

                    def to_tokens(job, dst, ready):
                        bank = full(job)
                        nc.vector.transpose(dst, D[bank][:, :]).then_inc(ready, 1)

                    def to_width(m, side):
                        src = (kt, qt)[side]
                        ins = nc.vector.transpose(kq[:, m * BC:(m + 1) * BC, side, :], group(src, m).rearrange("p (n d) -> p n d", d=DH))
                        if side:
                            ins.then_inc(kq_ready, 1)

                    def q_sum(m):
                        dve.wait_ge(q_sq, since(MS, m + 1))
                        step(nc.vector.tensor_reduce(ssq[:, m * BC:(m + 1) * BC], pt[:, m * BC:(m + 1) * BC, :], AX, ALU.add))

                    o_by_token(it, par)
                    if first and par == 0:
                        gate_up_bound()
                    to_tokens(JOB_K + 0, group(kt, 0), k_raw)
                    to_tokens(JOB_K + 1, group(kt, 1), k_raw)
                    o_sums(it, par, after, step)
                    to_tokens(JOB_K + 2, group(kt, 2), k_raw)
                    to_tokens(JOB_K + 3, group(kt, 3), k_raw)
                    n = o_scale(it, par, step)
                    dve.wait_ge(k_sq, since(1, 1))
                    k_sum = step(nc.vector.tensor_reduce(ssk[:, :], at[:, :].rearrange("p (n d) -> p n d", d=DH), AX, ALU.add))
                    after(k_sum)
                    k_sum = step(nc.vector.tensor_scalar(ssk[:, :], ssk[:, :], 1e-24, None, ALU.max))
                    after(k_sum)
                    root_guess(ssk[:, :], rk[:, :]).then_inc(ssk_ready, 1)
                    to_tokens(JOB_V + 0, group(vt, 0), v_raw)
                    nc.vector.transpose(kq_flat[:, 0:2048], o_tok).then_inc(ot_ready, 1)
                    for m in range(1, MS):
                        to_tokens(JOB_V + m, group(vt, m), v_raw)
                    dve.wait_ge(rk_ready, since(1, 1))
                    n = step(nc.vector.scalar_tensor_tensor(kt[:, :, :], kt[:, :, :], w_inv[:, 1:2], per_token(rk), ALU.mult, ALU.mult))
                    to_tokens(JOB_B, bt[:, :, :].rearrange("p c q -> p (c q)"), b_raw)
                    after(n)
                    dve.wait_ge(b_raw, since(1, 1))
                    nc.vector.tensor_tensor(tb[:, :, :], bt[:, :, 0:MS].rearrange("p c m -> p m c"),
                                            bt[:, :, MS:2 * MS].rearrange("p c m -> p m c"), ALU.add).then_inc(b_summed, 1)
                    dve.wait_ge(olo_ready, since(1, 1))
                    for m in range(MS):
                        to_width(m, 0)
                    dve.wait_ge(tb_ready, since(1, 1))
                    step(nc.vector.tensor_scalar(beta[:, :], tb[:, :, :].rearrange("p m c -> p (m c)"), 0.5, 0.5, ALU.mult, ALU.add))
                    if first and par == 0:
                        gate_up_scale()
                    for m in range(MS):
                        to_tokens(JOB_Q + m, group(qt, m), q_raw)
                        dve.wait_ge(q_raw, since(MS, m + 1))
                        to_width(m, 1)
                        if m:
                            q_sum(m - 1)
                    q_sum(MS - 1)
                    after(steps[0])
                    step(nc.vector.tensor_scalar(ssq[:, :], ssq[:, :], 1e-24, O_EPS, ALU.max, ALU.mult))

                    def fuse_tile(ic):
                        bank = full(gate_up_job(2 * ic + 1))
                        dve.wait_ge(sg_ready, since(IC, ic + 1))
                        dve.wait_ge(flo_ready, since(IC, max(0, ic + 1 - FUSE_RING)))
                        nc.vector.scalar_tensor_tensor(fuse[:, ic % FUSE_RING, :], D[bank][:, :], usf[:, ic:ic + 1], sg[:, ic % 2, :],
                                                       ALU.mult, ALU.mult).then_inc(f_ready, 1)

                    def read_gram(g):
                        dve.wait_ge(tiled_done, since(TILED, g + 1))
                        both = T[g % 4][:, :].rearrange("p (n a t) -> p n a t", n=8, a=2)
                        n0 = 8 * (g % 4)
                        step(nc.vector.tensor_tensor(a_nat[:, g // 4, n0:n0 + 8, :], both[:, :, 0, :],
                                                     beta[:, 8 * g:8 * g + 8].unsqueeze(2).to_broadcast([P, 8, CHUNK]), ALU.mult))
                        nc.vector.tensor_tensor(pt[:, 8 * g:8 * g + 8, :], both[:, :, 1, :],
                                                causal[:, :].unsqueeze(1).to_broadcast([P, 8, CHUNK]), ALU.mult).then_inc(p_ready, 1)

                    def by_problem(s):
                        after(steps[0])
                        nc.vector.transpose(m_prob[:, s], a_nat[:, s].rearrange("p n j -> p j n")).then_inc(m_ready, 1)

                    solved = [0, 0]
                    columns = lambda j: (CHUNK - 1 - j, min(j + 1, SPLIT))

                    def row_products(s, j):
                        shape = [P, *columns(j)]
                        tmp = outer_v[:, 256 * s:256 * s + shape[1] * shape[2]].rearrange("p (i c) -> p i c", c=shape[2])
                        after(solved[s])
                        solved[s] = step(nc.vector.tensor_tensor(tmp, m_prob[:, s, j, j + 1:].unsqueeze(2).to_broadcast(shape),
                                                                 t_prob[:, s, j, 0:shape[2]].unsqueeze(1).to_broadcast(shape), ALU.mult))

                    def off_rows(s, j):
                        rows, cols = columns(j)
                        tmp = outer_v[:, 256 * s:256 * s + rows * cols].rearrange("p (i c) -> p i c", c=cols)
                        rest = t_prob[:, s, j + 1:, 0:cols]
                        after(solved[s])
                        solved[s] = step(nc.vector.tensor_tensor(rest, rest, tmp, ALU.subtract))

                    def solve_steps(j0, j1):
                        for j in range(j0, j1):
                            row_products(0, j)
                            off_rows(0, j)

                    def t_transposed(s):
                        after(solved[s])
                        dve.wait_ge(t_ready, since(2, s + 1))
                        nc.vector.transpose(tt[:, 32 * s:32 * s + 32, :].rearrange("p n t -> p t n"), t_prob[:, s]).then_inc(tt_ready, 1)

                    def read_w(g):
                        dve.wait_ge(tiled_done, since(TILED, DONE_UW + g + 1))
                        nc.vector.transpose(kq[:, 8 * g:8 * g + 8, 0, :],
                                            T[g % 4][:, :].rearrange("p (n a d) -> p n a d", n=8, a=2)[:, :, 0, :]).then_inc(w_ready, 1)
                        if g in (2, 4, 6):
                            fuse_tile(7 + g // 2)

                    def add_out(j):
                        bank = full(JOB_WO + j)
                        y = xs[:, 1 - par, j, :]
                        nc.vector.scalar_tensor_tensor(y, D[bank][:, :], w_inv[:, 4:5], y, ALU.mult, ALU.add).then_inc(wo_added, 1)

                    for g in range(8):
                        read_gram(g)
                        if g in (2, 4, 6):
                            fuse_tile(g // 2 - 1)
                        if g == 3:
                            dve.wait_ge(zero_ready, since(1, 1))
                            for s in range(2):
                                ins = nc.vector.transpose(t_flat[:, 1024 * s:1024 * (s + 1):CHUNK + 1], beta[:, 32 * s:32 * s + 32])
                            ins.then_inc(diag_ready, 1)
                            by_problem(0)
                            dve.wait_ge(diag_ready, since(1, 1))
                            dve.wait_ge(m_ready, since(2, 1))
                        if g > 3:
                            solve_steps(LEAD * (g - 4) // 4, LEAD * (g - 3) // 4)
                    by_problem(1)
                    dve.wait_ge(acc_ready, since(TILES, 0))
                    dve.wait_ge(m_ready, since(2, 2))
                    for j in range(LEAD, CHUNK - 1 + LEAD):
                        sets = [(s, j - s * LEAD) for s in range(2) if j - s * LEAD < CHUNK - 1]
                        for s, i in sets:
                            row_products(s, i)
                        for s, i in sets:
                            off_rows(s, i)
                        if j in OUT_AT:
                            add_out(OUT_AT[j])
                        if j in FUSE_AT:
                            fuse_tile(FUSE_AT[j])
                        if j == CHUNK - 1:
                            t_transposed(0)
                        if j in W_AT:
                            read_w(W_AT[j])
                    t_transposed(1)

                    for g in range(len(W_AT), 8):
                        read_w(g)
                    fuse_tile(IC - 1)

                    def read_down(j):
                        bank = full(JOB_DN + j)
                        if j == 0:
                            dve.wait_ge(flo_ready, since(IC, IC))
                        dve.wait_ge(acc_ready, since(TILES, max(0, j - 1)))
                        nc.vector.tensor_tensor(fuse[:, j % 2, :], D[bank][:, :], ds_row[:, :], ALU.mult).then_inc(dn_ready, 1)

                    for c in range(STEPS):
                        halves = lambda bank: bank[:, :].rearrange("p (b m a t) -> p b m a t", b=BATCH, m=MS, a=2)
                        blocks = lambda tmp: tmp[:, 0:256].rearrange("p (b m t) -> p b m t", b=BATCH, m=MS)
                        dve.wait_ge(tiled_done, since(TILED, DONE_CHAIN + 2 * c + 1))
                        nc.vector.transpose(blocks(outer_v), halves(T[c % 2])[:, :, :, 0, :]).then_inc(ws_read, 1)
                        if c == 0:
                            dve.wait_ge(u_ready, since(8, 8))
                        dve.wait_ge(ws_read, since(STEPS, c + 1))
                        u = u_v[:, :, c]
                        nc.vector.tensor_tensor(u, u, blocks(outer_v), ALU.subtract).then_inc(r_ready, 1)
                        if c == 0:
                            dve.wait_ge(x_loaded, since(32, 64))
                            dve.nop(nofuse=True)
                            step(layer_norm_stats(0, 1 - par))
                            step(layer_norm_stats(1, 1 - par))
                        elif c == 1:
                            step(layer_norm_stats(2, 1 - par))
                            step(layer_norm_stats(3, 1 - par))
                        elif c == 2:
                            after(steps[0])
                            dve.nop(nofuse=True)
                            for j in range(TILES):
                                step(nc.vector.bn_aggr(mv[:, j, :], stats[:, j, :]))
                            after(steps[0])
                            nc.vector.tensor_scalar(var_e[:, :], mv[:, :, 1], LN_EPS, None, ALU.add).then_inc(var_ready, 1)
                        elif c in (3, 4):
                            dve.wait_ge(rstd_ready, since(1, 2))
                            for j in (2 * c - 6, 2 * c - 5):
                                layer_norm_apply(j, 1 - par).then_inc(xn_ready, 1)
                        elif c == STEPS - 1:
                            dve.wait_ge(xt_hi_ready, since(TILES, 2 * TILES))
                            low_xt(TILES - 1, XT_BANKS[TILES - 1])
                        dve.wait_ge(tiled_done, since(TILED, DONE_CHAIN + 2 * c + 2))
                        n = step(nc.vector.transpose(blocks(outer_p), halves(T[2 + c % 2])[:, :, :, 0, :]))
                        after(n)
                        nc.vector.tensor_tensor(state[:, :, :, :], state[:, :, :, :], blocks(outer_p), ALU.add).then_inc(s_ready, 1)
                        dve.wait_ge(qs_ready, since(STEPS, c + 1))
                        nc.vector.tensor_tensor(ot_v[:, :, c], ot_v[:, :, c], halves(T[2 + c % 2])[:, :, :, 1, :],
                                                ALU.add).then_inc(o_ready, 1)
                        if c in (2, 4, 6):
                            read_down(c // 2 - 1)
                        if c == STEPS - 2:
                            for j in range(TILES - 1):
                                dve.wait_ge(xt_hi_ready, since(TILES, TILES + j + 1))
                                low_xt(j, XT_BANKS[j])
                    read_down(3)
                    assert steps[0] == V_STEPS, steps

            two_spans(0, first=True)
            with dve.Fori(1, SPANS // 2) as it:
                two_spans(it)

            count = [0]

            def step(ins):
                ins.then_inc(v_step, 1)
                count[0] += 1
                return count[0]

            def after(n):
                dve.wait_ge(v_step, V_STEPS * SPANS + n)

            groups = [slice(m * TOK, (m + 1) * TOK) for m in range(MS)]
            dve.wait_ge(o_ready, STEPS * SPANS)
            for group in groups:
                nc.vector.transpose(o_tok[:, group], flat(qt)[:, group]).then_inc(otok_ready, 1)
            for m in range(MS):
                dve.wait_ge(o_sq, SPANS + m + 1)
                n = step(nc.vector.tensor_reduce(sso[:, m * BC:(m + 1) * BC], pt[:, m * BC:(m + 1) * BC, :], AX, ALU.add))
            after(n)
            after(step(nc.vector.scalar_tensor_tensor(sso[:, :], sso[:, :], 1.0 / DH, ssq[:, :], ALU.mult, ALU.add)))
            after(step(root_guess(sso[:, :], ro[:, :])))
            for n in range(NEWTONS):
                after(step(nc.vector.tensor_tensor(newton[:, :], ro[:, :], ro[:, :], ALU.mult)))
                after(step(nc.vector.scalar_tensor_tensor(newton[:, :], newton[:, :], -0.5, sso[:, :], ALU.mult, ALU.mult)))
                after(step(nc.vector.scalar_tensor_tensor(ro[:, :], newton[:, :], 1.5, ro[:, :], ALU.add, ALU.mult)))
            for m in range(MS):
                o3 = o_tok[:, groups[m]].rearrange("p (n d) -> p n d", d=DH)
                scale = ro[:, m * BC:(m + 1) * BC].unsqueeze(2).to_broadcast([P, BC, DH])
                after(step(nc.vector.scalar_tensor_tensor(o3, o3, q_scale[:, :], scale, ALU.mult, ALU.mult)))
                nc.vector.transpose(o_t[:, m, :], o_tok[:, groups[m]]).then_inc(ot_ready, 1)
            for m in range(MS):
                dve.wait_ge(ohi_ready, SPANS + m + 1)
                nc.vector.tensor_tensor(o_lo[:, m, :], o_t[:, m, :], o_hi[:, m, :], ALU.subtract).then_inc(olo_ready, 1)
            dve.wait_ge(acc_ready, TILES * SPANS)
            for j in range(TILES):
                dve.wait_ge(dense_done, XT_FIRST + SPANS * DENSE + j + 1)
                y = xs[:, 1, j, :]
                nc.vector.scalar_tensor_tensor(y, D[j][:, :], w_inv[:, 4:5], y, ALU.mult, ALU.add).then_inc(wo_added, 1)


_INS = ['L0_attn_hidden_states', 'L0_attn_Wq', 'L0_attn_Wk', 'L0_attn_Wv', 'L0_attn_Wb', 'L0_attn_o_norm_weight',
        'L0_attn_Wo', 'L0_ffn_gate_w', 'L0_ffn_up_w', 'L0_ffn_down_w', 'L0_ffn_gate_scale', 'L0_ffn_up_scale',
        'L0_ffn_down_scale']


def kernel(**inputs):
    import numpy as _np
    import concourse.bacc as _bacc
    from concourse import mybir as _mybir
    from concourse.bass_utils import run_bass_kernel_spmd as _run

    nc = _bacc.Bacc("TRN2", target_bir_lowering=False, num_devices=1)
    arrays, args = {}, []
    for name in _INS:
        a = _np.ascontiguousarray(inputs[name])
        arrays[f"in_{name}_dram"] = a
        args.append(nc.dram_tensor(f"in_{name}_dram", a.shape, _mybir.dt.from_np(a.dtype), kind="ExternalInput").ap())
    out = nc.dram_tensor("out_0_dram", (BATCH, LENGTH, DM), _mybir.dt.float32, kind="ExternalOutput").ap()
    delta_block_kernel(nc, *args, out)
    r = _run(nc, [arrays], core_ids=[0])
    return r.results[0]["out_0_dram"]
```
